# Optimizing a Trainium2 kernel written in Bass

```python
import numpy as np
import jax
import jax.numpy as jnp

def _softmax(x, axis=-1):
    return jax.nn.softmax(x, axis=axis)

def _gelu(x):
    return jax.nn.gelu(x, approximate=True)

def _silu(x):
    return jax.nn.silu(x)

def _sigmoid(x):
    return jax.nn.sigmoid(x)

def _layernorm(x, axis=-1, eps=1e-05):
    m = jnp.mean(x, axis=axis, keepdims=True)
    v = jnp.var(x, axis=axis, keepdims=True)
    return (x - m) / jnp.sqrt(v + eps)

def _scatter_add(tgt, idx, src, axis=0):
    return tgt.at[idx].add(src)

def _segment_sum(src, seg, n):
    return jax.ops.segment_sum(src, seg, n)
kernel_name = 'mk_adaln_d1_jaxref_r8_19a4df'

def setup_inputs(seed: int=0):
    np.random.seed(seed)
    _w = jnp.asarray

    def _L0_attn_setup():
        import jax, jax.numpy as jnp
        import numpy as np
        NUM_HEADS = 16
        THETA = 10000.0

        def _rotate_half(x):
            x = x.reshape(x.shape[:-1] + (-1, 2))
            x1, x2 = (x[..., 0], x[..., 1])
            return jnp.stack((-x2, x1), axis=-1).reshape(x.shape[:-2] + (-1,))

        def _rope(x):
            d_k = x.shape[-1]
            seq_len = x.shape[-2]
            inv_freq = 1.0 / THETA ** (jnp.arange(0, d_k, 2, dtype=jnp.float32) / d_k)
            pos = jnp.arange(seq_len, dtype=jnp.float32)
            theta = pos[:, None] * inv_freq[None, :]
            cos = jnp.repeat(jnp.cos(theta), 2, axis=-1)
            sin = jnp.repeat(jnp.sin(theta), 2, axis=-1)
            return x * cos + _rotate_half(x) * sin
        key = jax.random.key(seed)
        kx, kq, kk, kv, ko = jax.random.split(key, 5)
        B, S, D = (2, 256, 128)
        std = 1.0 / (2.0 * (2 * D) ** 0.5)
        return {'x': jax.random.normal(kx, (B, S, D), dtype=jnp.float32), 'Wq': jax.random.normal(kq, (D, D), dtype=jnp.float32) * std, 'Wk': jax.random.normal(kk, (D, D), dtype=jnp.float32) * std, 'Wv': jax.random.normal(kv, (D, D), dtype=jnp.float32) * std, 'Wo': jax.random.normal(ko, (D, D), dtype=jnp.float32) * std}
    _L0_attn_in = _L0_attn_setup()

    def _L0_ffn_setup():
        import math
        import jax, jax.numpy as jnp
        import numpy as np
        B, S, H = (4, 256, 128)
        E, K, I = (8, 2, 128)
        NSH = 2
        CF, RSF = (1.25, 1.0)
        key = jax.random.key(seed)
        ks = jax.random.split(key, 8)
        w = lambda k, sh: jax.random.normal(k, sh, dtype=jnp.float32) * 0.02
        return {'hidden_states': jax.random.normal(ks[0], (B, S, H), dtype=jnp.float32), 'gate_w': w(ks[1], (E, H)), 'we_gate': w(ks[2], (E, I, H)), 'we_up': w(ks[3], (E, I, H)), 'we_down': w(ks[4], (E, H, I)), 'ws_gate': w(ks[5], (NSH * I, H)), 'ws_up': w(ks[6], (NSH * I, H)), 'ws_down': w(ks[7], (H, NSH * I))}
    _L0_ffn_in = _L0_ffn_setup()
    _L0_c = _w((lambda *s: np.random.randn(*s).astype(np.float32) * 0.05)(16, 128))
    _L0_wmod = _w((lambda *s: np.random.randn(*s).astype(np.float32) * 0.05)(128, 6 * 128) * 128 ** (-0.5))
    _d = {'L0_attn_x': _L0_attn_in['x'], 'L0_attn_Wq': _L0_attn_in['Wq'], 'L0_attn_Wk': _L0_attn_in['Wk'], 'L0_attn_Wv': _L0_attn_in['Wv'], 'L0_attn_Wo': _L0_attn_in['Wo'], 'L0_ffn_gate_w': _L0_ffn_in['gate_w'], 'L0_ffn_we_gate': _L0_ffn_in['we_gate'], 'L0_ffn_we_up': _L0_ffn_in['we_up'], 'L0_ffn_we_down': _L0_ffn_in['we_down'], 'L0_ffn_ws_gate': _L0_ffn_in['ws_gate'], 'L0_ffn_ws_up': _L0_ffn_in['ws_up'], 'L0_ffn_ws_down': _L0_ffn_in['ws_down'], 'L0_c': _L0_c, 'L0_wmod': _L0_wmod}
    _x0 = _d['L0_attn_x']
    _d['L0_attn_x'] = jax.random.normal(jax.random.fold_in(jax.random.key(seed), 1), (16, 256, 128), dtype=_x0.dtype)
    del _x0
    return _d

def reference(L0_attn_x, L0_attn_Wq, L0_attn_Wk, L0_attn_Wv, L0_attn_Wo, L0_ffn_gate_w, L0_ffn_we_gate, L0_ffn_we_up, L0_ffn_we_down, L0_ffn_ws_gate, L0_ffn_ws_up, L0_ffn_ws_down, L0_c, L0_wmod):

    def _L0_attn_ref(x, Wq, Wk, Wv, Wo):
        import jax, jax.numpy as jnp
        import numpy as np
        NUM_HEADS = 16
        THETA = 10000.0

        def _rotate_half(x):
            x = x.reshape(x.shape[:-1] + (-1, 2))
            x1, x2 = (x[..., 0], x[..., 1])
            return jnp.stack((-x2, x1), axis=-1).reshape(x.shape[:-2] + (-1,))

        def _rope(x):
            d_k = x.shape[-1]
            seq_len = x.shape[-2]
            inv_freq = 1.0 / THETA ** (jnp.arange(0, d_k, 2, dtype=jnp.float32) / d_k)
            pos = jnp.arange(seq_len, dtype=jnp.float32)
            theta = pos[:, None] * inv_freq[None, :]
            cos = jnp.repeat(jnp.cos(theta), 2, axis=-1)
            sin = jnp.repeat(jnp.sin(theta), 2, axis=-1)
            return x * cos + _rotate_half(x) * sin
        B, S, D = x.shape
        H = NUM_HEADS
        d_k = D // H

        def split_heads(t):
            return t.reshape(B, S, H, d_k).transpose(0, 2, 1, 3)
        Q = split_heads(x @ Wq)
        K = split_heads(x @ Wk)
        V = split_heads(x @ Wv)
        Q = _rope(Q)
        K = _rope(K)
        scores = jnp.einsum('bhqd,bhkd->bhqk', Q, K) / jnp.sqrt(jnp.float32(d_k))
        causal = jnp.tril(jnp.ones((S, S), dtype=bool))
        scores = jnp.where(causal[None, None], scores, -jnp.inf)
        attn = jax.nn.softmax(scores, axis=-1)
        out = jnp.einsum('bhqk,bhkd->bhqd', attn, V)
        out = out.transpose(0, 2, 1, 3).reshape(B, S, D)
        return out @ Wo

    def _L0_ffn_ref(hidden_states, gate_w, we_gate, we_up, we_down, ws_gate, ws_up, ws_down):
        import math
        import jax, jax.numpy as jnp
        import numpy as np
        B, S, H = (4, 256, 128)
        E, K, I = (8, 2, 128)
        NSH = 2
        CF, RSF = (1.25, 1.0)
        orig_shape = hidden_states.shape
        x = hidden_states.reshape(-1, H)
        N = x.shape[0]
        logits = x.astype(jnp.float32) @ gate_w.astype(jnp.float32).T
        scores = jax.nn.softmax(logits, axis=-1)
        topk_w, topk_idx = jax.lax.top_k(scores, K)
        topk_w = topk_w / (topk_w.sum(-1, keepdims=True) + 1e-20) * RSF
        capacity = math.ceil(CF * N * K / E)
        flat = topk_idx.reshape(-1)
        one_hot = jax.nn.one_hot(flat, E, dtype=jnp.int32)
        pos = jnp.cumsum(one_hot, axis=0) - 1
        pos_tok = jnp.take_along_axis(pos, flat[:, None], axis=1)[:, 0]
        keep = (pos_tok < capacity).reshape(N, K)
        topk_w = topk_w * keep.astype(topk_w.dtype)
        comb = jnp.zeros((N, E), jnp.float32).at[jnp.arange(N)[:, None], topk_idx].add(topk_w)
        g = jnp.einsum('nh,eih->nei', x, we_gate)
        u = jnp.einsum('nh,eih->nei', x, we_up)
        eo = jnp.einsum('nei,ehi->neh', jax.nn.silu(g) * u, we_down)
        y = jnp.einsum('neh,ne->nh', eo, comb)
        sh = jax.nn.silu(x @ ws_gate.T) * (x @ ws_up.T) @ ws_down.T
        return (y + sh).reshape(orig_shape)
    x = L0_attn_x
    mod = (_silu(L0_c) @ L0_wmod).reshape(L0_c.shape[0], 6, 1, -1)
    sa, ca, ga, sb, cb, gb = (mod[:, 0], mod[:, 1], mod[:, 2], mod[:, 3], mod[:, 4], mod[:, 5])
    ga = (2 * (ga >= 0) - 1) * jnp.maximum(jnp.abs(ga), 0.25)
    gb = (2 * (gb >= 0) - 1) * jnp.maximum(jnp.abs(gb), 0.25)
    h = _layernorm(x, axis=-1) * (1 + ca) + sa
    x = x + ga * _L0_attn_ref(h, L0_attn_Wq, L0_attn_Wk, L0_attn_Wv, L0_attn_Wo)
    h = _layernorm(x, axis=-1) * (1 + cb) + sb
    x = x + gb * _L0_ffn_ref(h, L0_ffn_gate_w, L0_ffn_we_gate, L0_ffn_we_up, L0_ffn_we_down, L0_ffn_ws_gate, L0_ffn_ws_up, L0_ffn_ws_down)
    return x

_drawn_inputs = setup_inputs


def setup_inputs(seed=0):
    import zlib

    import numpy as np

    out = dict(_drawn_inputs(seed))
    spreads = {}
    factors = {'L0_attn_Wq': 8.0,
     'L0_attn_Wk': 8.0,
     'L0_attn_Wv': 8.0,
     'L0_attn_Wo': 8.0,
     'L0_ffn_gate_w': 8.0,
     'L0_ffn_we_gate': 8.0,
     'L0_ffn_we_up': 8.0,
     'L0_ffn_we_down': 8.0,
     'L0_ffn_ws_gate': 8.0,
     'L0_ffn_ws_up': 8.0,
     'L0_ffn_ws_down': 8.0,
     'L0_c': 8.0,
     'L0_wmod': 8.0}
    for name, (base, spread) in spreads.items():
        noise = np.random.default_rng([zlib.crc32(name.encode()), seed]).standard_normal(out[name].shape)
        drawn = base * np.exp(spread * noise) if base else spread * noise
        out[name] = jnp.asarray(drawn.astype(out[name].dtype))
    for name, factor in factors.items():
        out[name] = (out[name] * factor).astype(out[name].dtype)
    return out
```

```python
from contextlib import ExitStack

import numpy as np

import concourse.bass as bass
from concourse import mybir

F32 = mybir.dt.float32
F32R = mybir.dt.float32r
BF16 = mybir.dt.bfloat16
ALU = mybir.AluOpType
ACT = mybir.ActivationFunctionType
AX_X = mybir.AxisListType.X

P = 128
B, S, D = 16, 256, 128
NT = S // P
H, DK = 16, 8
NA, NG = 4, 4
E, I = 8, 128
NSH = 2
NX = NSH + E
CAP = -(-5 * B * S * 2 // (4 * E))
W = 32
HI0, MID, LAST, MAXC = 0, DK, 2 * DK, 3 * DK
KS = 3 * DK
KM = KS + 2
NR = 12
NP = 4
EPS = 1e-5
NEG = -1e30
SCALE = float(DK) ** -0.5


class Batch:

    def __init__(self, i, c):
        self.i, self.c, self.p = i, c, c % 2

    def shift(self, n):
        return Batch(self.i, self.c + n)

    @property
    def index(self):
        return self.i * 2 + self.c

    def after(self, n, k):
        return self.i * (2 * n) + (n * self.c + k)

    def nth_of_parity(self, n, k):
        return self.i * n + (n * (self.c // 2) + k)


def step_order():
    order = [("load", 0), ("norm_out", 0), ("max", 0), ("max", 1), ("wo", 0), ("max", 2), ("max", 3),
             ("residual", 0), ("max", 4), ("max", 5), ("max", 6), ("ln2", 0), ("max", 7), ("max", 8),
             ("logits", 0), ("max", 9), ("route", 0), ("max", 10), ("counts", 0), ("max", 11), ("comb", 0),
             ("shift", 0), ("ffn", 0), ("ln1", 0), ("exp", 0), ("ffn", 1), ("qkv", 0)]
    f = 2
    for r in range(1, NR):
        order.append(("exp", r))
        if r == 3:
            order.append(("stack", 0))
        if f <= NX:
            order.append(("ffn", f))
            f += 1
    order.append(("final", 0))
    return order


STEP = step_order()


def has(stage, front, mid, tail):
    if stage in ("ln1", "qkv", "stack", "load"):
        return front is not None
    if stage in ("max", "shift", "exp"):
        return mid is not None
    return tail is not None


def run_steps(eng, step):
    at = lambda b: Batch(b // 2, b % 2) if 0 <= b < B else None
    for s in range(-1, 2):
        step(at(s + 1), at(s), at(s - 1))
    with eng.Fori(0, (B - 4) // 2) as i:
        for c in (2, 3):
            step(Batch(i, c + 1), Batch(i, c), Batch(i, c - 1))
    for s in range(B - 2, B + 1):
        step(at(s + 1), at(s), at(s - 1))


def before(b, n=1):
    if isinstance(b.i, int) and 2 * b.i + b.c < n:
        return None
    return b.shift(-n)


def score_round(r, first):
    if first:
        return (r, range(NA), 0) if r < 4 else ((r - 4) // 2, range(2 * (r % 2), 2 * (r % 2) + 2), 1)
    return (r // 2, range(2 * (r % 2), 2 * (r % 2) + 2), 0) if r < 8 else (r - 8, range(NA), 1)


def block_kernel(nc, x, wqkv, wo, gate_w, wgu, wd, c, wmod, rope, out):
    gate_rows = nc.dram_tensor("gate_rows", [B, 2 * D], F32, kind="Internal").ap()
    with ExitStack() as ctx:
        def sb(name, shape, dt=F32):
            return ctx.enter_context(nc.sbuf_tensor(name, shape, dt))

        def sem(name):
            return ctx.enter_context(nc.semaphore(name))

        ps_score = [ctx.enter_context(nc.psum_tensor(f"ps_score{n}", [P, 512], F32)) for n in range(2)]
        ps_gu = [ctx.enter_context(nc.psum_tensor(f"ps_gu{n}", [P, 2, S], F32)) for n in range(2)]
        ps_y = ctx.enter_context(nc.psum_tensor("ps_y", [P, NT, 2 * D], F32))
        ps_t = ctx.enter_context(nc.psum_tensor("ps_t", [P, 2, 512], F32))
        ps_o = ctx.enter_context(nc.psum_tensor("ps_o", [P, 2, S], F32))

        wqkv_sb = sb("wqkv_sb", [P, 3 * D])
        wo_sb = sb("wo_sb", [P, 2, D])
        gw_sb = sb("gw_sb", [P, E])
        wgu_sb = sb("wgu_sb", [P, NX * 2 * I])
        wgu_hi = sb("wgu_hi", [P, NX * 2 * I], F32R)
        wgu_lo = sb("wgu_lo", [P, NX * 2 * I], F32R)
        wd_sb = sb("wd_sb", [P, NX * D])
        wmod_sb = sb("wmod_sb", [P, 6 * D])
        rope_sb = sb("rope_sb", [P, NT, 2, DK])
        ident = sb("ident", [P, P])
        ident_b = sb("ident_b", [P, P], BF16)
        mask_q = sb("mask_q", [P, NA * P], BF16)
        mask_k = sb("mask_k", [P, NA * P], BF16)
        before_b = sb("before_b", [P, P], BF16)
        ones_b = sb("ones_b", [P, P], BF16)
        lower = sb("lower", [P, E, E])
        upper = sb("upper", [P, E, E])
        minus_half = sb("minus_half", [P, NT])
        c_sb = sb("c_sb", [B, D])
        c_th = sb("c_th", [B, D])
        c_silu = sb("c_silu", [B, D])
        cT = sb("cT", [P, B])
        mod = sb("mod", [P, B, 4])
        gate_raw = sb("gate_raw", [B, 2 * D])
        gate_sign = sb("gate_sign", [B, 2 * D])
        gate_mag = sb("gate_mag", [B, 2 * D])
        x_sb = [sb(f"x_sb{n}", [P, NT, D]) for n in range(2)]
        gates = [sb(f"gates{n}", [P, 2 * D]) for n in range(2)]
        st1 = sb("st1", [P, NT, 6])
        mv1 = sb("mv1", [P, NT, 2])
        ve1 = sb("ve1", [P, NT])
        rstd1 = sb("rstd1", [P, NT])
        xn1 = sb("xn1", [P, NT, D])
        h1T = sb("h1T", [P, S])
        qk_cos = sb("qk_cos", [P, NT, 2 * D])
        qk_sin = sb("qk_sin", [P, NT, 2 * D])
        qk = sb("qk", [P, NT, 2 * D])
        stack = sb("stack", [P, NT, 2 * H * W], F32R)
        v_ones = [sb(f"v_ones{n}", [P, NT, H, W]) for n in range(2)]
        qT = [sb(f"qT{n}", [P, NA, S], F32R) for n in range(2)]
        kT = [sb(f"kT{n}", [P, NA, S], F32R) for n in range(2)]
        mx = sb("mx", [P, NT, H])
        probs = [sb(f"probs{n}", [P, 512]) for n in range(NP)]
        den = sb("den", [P, 2, S])
        rden = sb("rden", [P, 2, S])
        onT = sb("onT", [P, 2, S])
        gated = sb("gated", [P, NT, D])
        x1 = sb("x1", [P, NT, D])
        st2 = sb("st2", [P, NT, 6])
        mv2 = sb("mv2", [P, NT, 2])
        ve2 = sb("ve2", [P, NT])
        rstd2 = sb("rstd2", [P, NT])
        xn2 = sb("xn2", [P, NT, D])
        h2T = sb("h2T", [P, S])
        h2_hi = sb("h2_hi", [P, S], F32R)
        h2_lo = sb("h2_lo", [P, S], F32R)
        lmax = sb("lmax", [P, NT])
        ldif = sb("ldif", [P, NT, E])
        ex = sb("ex", [P, NT, E])
        ge = sb("ge", [P, NT, E, E])
        gt = sb("gt", [P, NT, E, E])
        ge_l = sb("ge_l", [P, NT, E, E])
        gt_u = sb("gt_u", [P, NT, E, E])
        beats = sb("beats", [P, NT, E, E])
        rank = sb("rank", [P, NT, E])
        sel = sb("sel", [P, NT, E])
        sel_b = sb("sel_b", [P, NT, E], BF16)
        sel_past = sb("sel_past", [P, E], BF16)
        esum = sb("esum", [P, NT])
        esel = sb("esel", [P, NT, E])
        wsum = sb("wsum", [P, NT])
        wden = sb("wden", [P, NT])
        wrec = sb("wrec", [P, NT])
        ekeep = sb("ekeep", [P, NT, E])
        comb = sb("comb", [P, NT, E])
        th = [sb(f"th{n}", [P, S]) for n in range(2)]
        silu = [sb(f"silu{n}", [P, S]) for n in range(2)]
        hid = [sb(f"hid{n}", [P, S]) for n in range(2)]
        acc = sb("acc", [P, NT, D])
        gacc = sb("gacc", [P, NT, D])
        out_sb = [sb(f"out_sb{n}", [P, NT, D]) for n in range(2)]

        passed = sem("passed")
        c_loaded, weights_loaded, ffn_loaded = sem("c_loaded"), sem("weights_loaded"), sem("ffn_loaded")
        c_tanh, c_done, cT_ready, cT_copied, mod_ready, mod_stored = (
            sem("c_tanh"), sem("c_done"), sem("cT_ready"), sem("cT_copied"), sem("mod_ready"), sem("mod_stored"))
        setup_pool, setup_dve, gates_computed, gates_written = (
            sem("setup_pool"), sem("setup_dve"), sem("gates_computed"), sem("gates_written"))
        consts_ready, dve_consts, ffn_split = sem("consts_ready"), sem("dve_consts"), sem("ffn_split")
        x_loaded = [sem(f"x_loaded{n}") for n in range(2)]
        gates_loaded = [sem(f"gates_loaded{n}") for n in range(2)]
        ln1_stats, ln1_mv, ln1_var, ln1_rstd, xn1_ready = (
            sem("ln1_stats"), sem("ln1_mv"), sem("ln1_var"), sem("ln1_rstd"), sem("xn1_ready"))
        xT1_ready, h1_copied, qkv_ready = sem("xT1_ready"), sem("h1_copied"), sem("qkv_ready")
        qkv_read, rope_done, hi_done, lo_done, hi_again = (
            sem("qkv_read"), sem("rope_done"), sem("hi_done"), sem("lo_done"), sem("hi_again"))
        st_ready, st_copied = sem("st_ready"), sem("st_copied")
        max_scores, max_taken = sem("max_scores"), sem("max_taken")
        max_hi, max_lo, q2_ready, q2_copied = sem("max_hi"), sem("max_lo"), sem("q2_ready"), sem("q2_copied")
        exp_scores, exp_done, pv_done = sem("exp_scores"), sem("exp_done"), sem("pv_done")
        den_moved, den_rec, on_ready, wo_ready, gated_ready, x1_ready = (
            sem("den_moved"), sem("den_rec"), sem("on_ready"), sem("wo_ready"), sem("gated_ready"), sem("x1_ready"))
        ln2_stats, ln2_mv, ln2_var, ln2_rstd, xn2_ready = (
            sem("ln2_stats"), sem("ln2_mv"), sem("ln2_var"), sem("ln2_rstd"), sem("xn2_ready"))
        xT2_ready, h2_copied, h2_hi_done, h2_lo_done = (
            sem("xT2_ready"), sem("h2_copied"), sem("h2_hi_done"), sem("h2_lo_done"))
        logits_ready, lmax_done, ldif_done, route_exp = (
            sem("logits_ready"), sem("lmax_done"), sem("ldif_done"), sem("route_exp"))
        rank_steps, sel_ready, counts_ready, comb_steps = (
            sem("rank_steps"), sem("sel_ready"), sem("counts_ready"), sem("comb_steps"))
        gu_ready, th_done, silu_done, hid_ready = (
            sem("gu_ready"), sem("th_done"), sem("silu_done"), sem("hid_ready"))
        y_ready, y_used = sem("y_ready"), sem("y_used")
        gacc_ready, out_ready = sem("gacc_ready"), sem("out_ready")
        out_stored = [sem(f"out_stored{n}") for n in range(2)]

        heads = lambda t: t.rearrange("p t (h w) -> p t h w", w=W)
        NY = NX - 1
        SETUP_LOADS = 6

        block = ctx.enter_context(nc.Block())

        def wait_apart(eng, signal, value):
            eng.wait_ge(signal, value)
            eng.sem_inc(passed, 1)

        @block.sync
        def _(sp):
            sp.dma_start(c_sb[:, :], c).then_inc(c_loaded, 16)
            for dst, src in ((wmod_sb[:, :], wmod), (wqkv_sb[:, :], wqkv),
                             (rope_sb[:, :, :, :], rope.rearrange("(t p) a d -> p t a d", p=P)),
                             (wo_sb[:, :, :], wo.rearrange("j p n -> p j n")), (gw_sb[:, :], gate_w),
                             ):
                sp.dma_start(dst, src).then_inc(weights_loaded, 16)
            sp.wait_ge(gates_computed, 1)
            sp.dma_start(gate_rows, gate_mag[:, :]).then_inc(gates_written, 16)
            sp.wait_ge(gates_written, 16)
            sp.dma_start(wgu_sb[:, :], wgu).then_inc(ffn_loaded, 16)
            sp.dma_start(wd_sb[:, :], wd).then_inc(ffn_loaded, 16)

            def step(front, mid, tail):
                for stage, k in STEP:
                    if not has(stage, front, mid, tail):
                        continue
                    if stage == "load":
                        b, old = front, before(front, 2)
                        if old is not None:
                            sp.wait_ge(x1_ready, old.after(1, 1))
                        sp.dma_start(x_sb[b.p][:, :, :],
                                     x[bass.ds(b.index, 1)].rearrange("o (t p) d -> p (o t) d", p=P)
                                     ).then_inc(x_loaded[b.p], 16)
                    if stage == "final":
                        b = tail
                        sp.wait_ge(out_ready, b.after(1, 1))
                        sp.dma_start(out[bass.ds(b.index, 1)].rearrange("o (t p) d -> p (o t) d", p=P),
                                     out_sb[b.p][:, :, :]).then_inc(out_stored[b.p], 16)
                if front is not None:
                    b, old = front, before(front, 2)
                    if old is not None:
                        sp.wait_ge(out_ready, old.after(1, 1))
                    sp.dma_start(gates[b.p][:, :],
                                 gate_rows[bass.ds(b.index, 1)].to_broadcast([P, 2 * D])
                                 ).then_inc(gates_loaded[b.p], 16)

            run_steps(sp, step)
            for n in range(2):
                sp.wait_ge(out_stored[n], 16 * (B // 2))

        @block.gpsimd
        def _(pool):
            n = 0

            def link(ins):
                nonlocal n
                n += 1
                ins.then_inc(setup_pool, 1)
                pool.wait_ge(setup_pool, n)

            g = nc.gpsimd
            link(g.memset(ident[:, :], 0.0))
            link(g.affine_select(out=ident[:, :], in_=ident[:, :], compare_op=ALU.not_equal, fill=1.0,
                                 base=0, pattern=[[-1, P]], channel_multiplier=1))
            g.tensor_copy(ident_b[:, :], ident[:, :]).then_inc(consts_ready, 1)
            g.memset(minus_half[:, :], -0.5).then_inc(consts_ready, 1)
            link(g.memset(mask_q[:, :], 0.0))
            g.affine_select(out=mask_q[:, :], in_=mask_q[:, :], compare_op=ALU.is_ge, fill=NEG, base=0,
                            pattern=[[0, NA], [-1, P]], channel_multiplier=1).then_inc(consts_ready, 1)
            link(g.memset(mask_k[:, :], 0.0))
            g.affine_select(out=mask_k[:, :], in_=mask_k[:, :], compare_op=ALU.is_ge, fill=NEG, base=0,
                            pattern=[[0, NA], [1, P]], channel_multiplier=-1).then_inc(consts_ready, 1)
            link(g.memset(before_b[:, :], 1.0))
            g.affine_select(out=before_b[:, :], in_=before_b[:, :], compare_op=ALU.is_gt, fill=0.0, base=0,
                            pattern=[[1, P]], channel_multiplier=-1).then_inc(consts_ready, 1)
            link(g.memset(lower[:, :, :], 1.0))
            g.affine_select(out=lower[:, :, :], in_=lower[:, :, :], compare_op=ALU.is_gt, fill=0.0, base=0,
                            pattern=[[1, E], [-1, E]], channel_multiplier=0).then_inc(consts_ready, 1)
            link(g.memset(upper[:, :, :], 1.0))
            g.affine_select(out=upper[:, :, :], in_=upper[:, :, :], compare_op=ALU.is_gt, fill=0.0, base=0,
                            pattern=[[-1, E], [1, E]], channel_multiplier=0).then_inc(consts_ready, 1)

            def normalise(b, stats, mv, ve, rstd, src, dst, var_done, rstd_done, done):
                wait_apart(pool, stats, b.after(1, 1))
                g.tensor_scalar(ve[:, :], mv[:, :, 1], EPS, None, ALU.add).then_inc(var_done, 1)
                pool.wait_ge(var_done, b.after(1, 1))
                g.tensor_tensor(rstd[:, :], ve[:, :], minus_half[:, :], ALU.pow).then_inc(rstd_done, 1)
                wait_apart(pool, rstd_done, b.after(1, 1))
                for t in range(NT):
                    g.tensor_scalar(dst[:, t, :], src[:, t, :], mv[:, t, 0:1], rstd[:, t:t + 1],
                                    ALU.subtract, ALU.mult).then_inc(done, 1)

            def step(front, mid, tail):
                for stage, k in STEP:
                    if not has(stage, front, mid, tail):
                        continue
                    if stage == "ln1":
                        normalise(front, ln1_mv, mv1, ve1, rstd1, x_sb[front.p], xn1,
                                  ln1_var, ln1_rstd, xn1_ready)
                    if stage == "ln2":
                        normalise(tail, ln2_mv, mv2, ve2, rstd2, x1, xn2, ln2_var, ln2_rstd, xn2_ready)
                    if stage == "qkv":
                        wait_apart(pool, hi_done, front.after(1, 1))
                        for o, slot in ((0, MID), (H, LAST)):
                            v = heads(stack[:, :, :])
                            g.tensor_copy(v[:, :, o:o + H, slot:slot + DK].bitcast(F32),
                                          v[:, :, o:o + H, HI0:HI0 + DK].bitcast(F32)).then_inc(hi_again, 1)

            run_steps(pool, step)

        @block.scalar
        def _(act):
            s = nc.scalar
            act.wait_ge(c_loaded, 16)
            s.activation(c_th[:, :], c_sb[:, :], ACT.Tanh, scale=0.5).then_inc(c_tanh, 1)

            def transposed(dst, src, b, which, done):
                m = mod[:, bass.ds(b.index, 1), :]
                s.activation(dst, src, ACT.Identity, scale=m[:, :, which:which + 1].rearrange("p o k -> p (o k)"),
                             bias=m[:, :, which + 1:which + 2].rearrange("p o k -> p (o k)")).then_inc(done, 1)

            def step(front, mid, tail):
                for stage, k in STEP:
                    if not has(stage, front, mid, tail):
                        continue
                    if stage == "ln1":
                        if isinstance(front.i, int) and front.index == 0:
                            act.wait_ge(mod_stored, 1)
                        act.wait_ge(xT1_ready, front.after(1, 1))
                        transposed(h1T[:, :], ps_t[:, 0, 0:S], front, 0, h1_copied)
                    if stage == "stack":
                        for f in range(4):
                            act.wait_ge(st_ready, front.after(4, f + 1))
                            dst = (kT, kT, qT, qT)[f][front.p][:, 2 * (f % 2):2 * (f % 2) + 2, :]
                            s.activation(dst, ps_t[:, f % 2, :].rearrange("p (a q) -> p a q", a=2),
                                         ACT.Copy).then_inc(st_copied, 1)
                    if stage == "shift":
                        for f in range(2):
                            act.wait_ge(q2_ready, mid.after(2, f + 1))
                            s.activation(qT[mid.p][:, 2 * f:2 * f + 2, :],
                                         ps_t[:, f, :].rearrange("p (a q) -> p a q", a=2),
                                         ACT.Copy).then_inc(q2_copied, 1)
                    if stage == "exp":
                        act.wait_ge(exp_scores, mid.after(NR, k + 1))
                        if k >= NP:
                            act.wait_ge(pv_done, mid.after(NR, k - NP + 1))
                        elif before(mid) is not None:
                            act.wait_ge(pv_done, mid.after(NR, k - NP + 1))
                        s.activation(probs[k % NP][:, :], ps_score[k % 2][:, :], ACT.Exp,
                                     scale=SCALE).then_inc(exp_done, 1)
                    if stage == "ln2":
                        act.wait_ge(xT2_ready, tail.after(1, 1))
                        transposed(h2T[:, :], ps_t[:, 1, 0:S], tail, 2, h2_copied)
                        transposed(h2_hi[:, :], ps_t[:, 1, 0:S], tail, 2, h2_hi_done)
                    if stage == "route":
                        act.wait_ge(ldif_done, tail.after(1, 1))
                        s.activation(ex[:, :, :], ldif[:, :, :], ACT.Exp).then_inc(route_exp, 1)
                    if stage == "ffn" and k < NX:
                        act.wait_ge(gu_ready, tail.after(NX, k + 1))
                        if k >= 2 or before(tail) is not None:
                            act.wait_ge(silu_done, tail.after(NX, k - 1))
                        s.activation(th[k % 2][:, :], ps_gu[k % 2][:, 0, :], ACT.Tanh,
                                     scale=0.5).then_inc(th_done, 1)

            run_steps(act, step)

        @block.vector
        def _(dve):
            v = nc.vector
            n = 0

            def link(ins):
                nonlocal n
                n += 1
                ins.then_inc(setup_dve, 1)
                dve.wait_ge(setup_dve, n)

            dve.wait_ge(c_tanh, 1)
            link(v.tensor_scalar(c_th[:, :], c_th[:, :], 1.0, 0.5, ALU.add, ALU.mult))
            v.tensor_tensor(c_silu[:, :], c_th[:, :], c_sb[:, :], ALU.mult).then_inc(c_done, 1)
            link(v.memset(stack[:, :, :].bitcast(F32), 0.0))
            v.memset(heads(stack[:, :, :])[:, :, H:2 * H, MAXC:MAXC + 2].bitcast(F32), 1.0).then_inc(dve_consts, 1)
            for n2 in range(2):
                link(v.memset(v_ones[n2][:, :, :, :], 0.0))
                pair = v_ones[n2][:, :, :, :].rearrange("p t (c o) w -> p t c o w", o=2)
                for o in range(2):
                    for t in range(NT):
                        v.memset(pair[:, t, :, o, 16 * o + DK:16 * o + 2 * DK], 1.0).then_inc(dve_consts, 1)
            v.memset(ones_b[:, :], 1.0).then_inc(dve_consts, 1)
            v.memset(sel_past[:, :], 0.0).then_inc(dve_consts, 1)
            dve.wait_ge(cT_ready, 1)
            v.tensor_copy(cT[:, :], ps_o[:, 0, 0:B]).then_inc(cT_copied, 1)
            dve.wait_ge(mod_ready, 1)
            mv = ps_o[:, 1, 0:4 * B].rearrange("p (k b) -> p b k", b=B)
            link(v.tensor_copy(gate_raw[:, :], ps_o[0:B, 0, 0:2 * D]))
            for k in range(4):
                ins = v.tensor_scalar(mod[:, :, k], mv[:, :, k], 1.0 if k % 2 == 0 else 0.0, None, ALU.add)
                if k < 3:
                    link(ins)
            ins.then_inc(mod_stored, 1)
            link(v.tensor_scalar(gate_sign[:, :], gate_raw[:, :], 0.0, 2.0, ALU.is_ge, ALU.mult))
            link(v.tensor_scalar(gate_mag[:, :], gate_raw[:, :], -1.0, None, ALU.mult))
            link(v.tensor_tensor(gate_raw[:, :], gate_mag[:, :], gate_raw[:, :], ALU.max))
            link(v.tensor_scalar(gate_raw[:, :], gate_raw[:, :], 0.25, None, ALU.max))
            v.scalar_tensor_tensor(gate_mag[:, :], gate_sign[:, :], -1.0, gate_raw[:, :],
                                   ALU.add, ALU.mult).then_inc(gates_computed, 1)

            def layer_stats(b, src, st, mv, stats, done):
                for t in range(NT):
                    v.bn_stats(st[:, t, :], src[:, t, :]).then_inc(stats, 1)
                wait_apart(dve, stats, b.after(NT, NT))
                for t in range(NT):
                    ins = v.bn_aggr(mv[:, t, :], st[:, t, :])
                ins.then_inc(done, 1)

            def step(front, mid, tail):
                for stage, k in STEP:
                    if not has(stage, front, mid, tail):
                        continue
                    if stage == "ln1":
                        b = front
                        dve.wait_ge(x_loaded[b.p], b.nth_of_parity(16, 16))
                        layer_stats(b, x_sb[b.p], st1, mv1, ln1_stats, ln1_mv)
                    if stage == "qkv":
                        rope_and_split(front)
                    if stage == "max":
                        b = mid
                        g, blocks, t = score_round(k, True)
                        dve.wait_ge(max_scores, b.after(NR, k + 1))
                        v.reduce_max(mx[:, t, :].rearrange("p (a g) -> p a g", g=NG)[:, blocks[0]:blocks[-1] + 1, g],
                                     ps_score[k % 2][:, :].rearrange("p (a q) -> p a q", a=len(blocks)),
                                     AX_X).then_inc(max_taken, 1)
                    if stage == "shift":
                        b = mid
                        q = heads(stack[:, :, :])[:, :, 0:H, :]
                        dve.wait_ge(max_taken, b.after(NR, NR))
                        v.tensor_scalar(q[:, :, :, MAXC], mx[:, :, :], -1.0, None, ALU.mult).then_inc(max_hi, 1)
                        dve.wait_ge(max_hi, b.after(1, 1))
                        v.scalar_tensor_tensor(q[:, :, :, MAXC + 1], mx[:, :, :], -1.0,
                                               q[:, :, :, MAXC].bitcast(F32), ALU.mult,
                                               ALU.subtract).then_inc(max_lo, 1)
                    if stage == "norm_out":
                        b = tail
                        wait_apart(dve, pv_done, b.after(NR, NR))
                        mask = [16 * (m // 16) + DK + m % DK for m in range(32)]
                        v.stream_shuffle(den[:, :, :], ps_o[:, :, :], mask).then_inc(den_moved, 1)
                        dve.wait_ge(den_moved, b.after(1, 1))
                        v.reciprocal(rden[:, :, :], den[:, :, :]).then_inc(den_rec, 1)
                        dve.wait_ge(den_rec, b.after(1, 1))
                        v.tensor_tensor(onT[:, :, :], ps_o[:, :, :], rden[:, :, :], ALU.mult).then_inc(on_ready, 1)
                    if stage == "residual":
                        b = tail
                        dve.wait_ge(gates_loaded[b.p], b.nth_of_parity(16, 16))
                        dve.wait_ge(wo_ready, b.after(1, 1))
                        ga = gates[b.p][:, 0:D].unsqueeze(1).to_broadcast([P, NT, D])
                        v.tensor_tensor(gated[:, :, :], ps_t[:, 0, 0:S].rearrange("p (t d) -> p t d", t=NT),
                                        ga, ALU.mult).then_inc(gated_ready, 1)
                        dve.wait_ge(gated_ready, b.after(1, 1))
                        v.tensor_tensor(x1[:, :, :], gated[:, :, :], x_sb[b.p][:, :, :], ALU.add
                                        ).then_inc(x1_ready, 1)
                        dve.wait_ge(x1_ready, b.after(1, 1))
                        layer_stats(b, x1, st2, mv2, ln2_stats, ln2_mv)
                    if stage == "logits":
                        b = tail
                        dve.wait_ge(h2_copied, b.after(1, 1))
                        dve.wait_ge(h2_hi_done, b.after(1, 1))
                        v.tensor_tensor(h2_lo[:, :], h2T[:, :], h2_hi[:, :].bitcast(F32),
                                        ALU.subtract).then_inc(h2_lo_done, 1)
                        dve.wait_ge(logits_ready, b.after(1, 1))
                        lg = ps_t[:, 0, 0:NT * E].rearrange("p (t e) -> p t e", t=NT)
                        v.reduce_max(lmax[:, :], lg, AX_X).then_inc(lmax_done, 1)
                        dve.wait_ge(lmax_done, b.after(1, 1))
                        v.tensor_tensor(ldif[:, :, :], lg, lmax[:, :].unsqueeze(2).to_broadcast([P, NT, E]),
                                        ALU.subtract).then_inc(ldif_done, 1)
                    if stage == "route":
                        route(tail)
                    if stage == "comb":
                        combine_weights(tail)
                    if stage == "ffn":
                        ffn(tail, k)
                    if stage == "final":
                        b = tail
                        old = before(b, 2)
                        dve.wait_ge(y_used, b.after(NY, NY))
                        gb = gates[b.p][:, D:2 * D].unsqueeze(1).to_broadcast([P, NT, D])
                        v.tensor_tensor(gacc[:, :, :], acc[:, :, :], gb, ALU.mult).then_inc(gacc_ready, 1)
                        dve.wait_ge(gacc_ready, b.after(1, 1))
                        if old is not None:
                            dve.wait_ge(out_stored[b.p], old.nth_of_parity(16, 16))
                        v.tensor_tensor(out_sb[b.p][:, :, :], gacc[:, :, :], x1[:, :, :],
                                        ALU.add).then_inc(out_ready, 1)

            def rope_and_split(b):
                st = heads(stack[:, :, :])
                raw = ps_t[:, :, 0:2 * D].rearrange("p t (h d) -> p t h d", d=DK)
                cos = rope_sb[:, :, 0, :].unsqueeze(2).to_broadcast([P, NT, 2 * H, DK])
                sin = rope_sb[:, :, 1, :].unsqueeze(2).to_broadcast([P, NT, 2 * H, DK])
                dve.wait_ge(qkv_ready, b.after(1, 1))
                v.tensor_tensor(qk_cos[:, :, :].rearrange("p t (h d) -> p t h d", d=DK), raw, cos,
                                ALU.mult).then_inc(qkv_read, 1)
                sn = qk_sin[:, :, :].rearrange("p t (h d) -> p t h d", d=DK)
                for o in range(2):
                    v.tensor_tensor(sn[:, :, :, o::2], raw[:, :, :, 1 - o::2], sin[:, :, :, o::2],
                                    ALU.mult).then_inc(qkv_read, 1)
                if before(b, 2) is not None:
                    dve.wait_ge(pv_done, before(b, 2).after(NR, NR))
                val = ps_t[:, :, 2 * D:3 * D].rearrange("p t (c o d) -> p t c o d", o=2, d=DK)
                vo = v_ones[b.p][:, :, :, :].rearrange("p t (c o) w -> p t c o w", o=2)
                for o in range(2):
                    v.tensor_copy(vo[:, :, :, o, 16 * o:16 * o + DK], val[:, :, :, o, :]).then_inc(qkv_read, 1)
                dve.wait_ge(qkv_read, b.after(5, 3))
                v.tensor_tensor(qk[:, :, :], qk_cos[:, :, :], qk_sin[:, :, :], ALU.add).then_inc(rope_done, 1)
                dve.wait_ge(rope_done, b.after(1, 1))
                if before(b) is not None:
                    dve.wait_ge(q2_ready, before(b).after(2, 2))
                qk4 = qk[:, :, :].rearrange("p t (h d) -> p t h d", d=DK)
                v.tensor_copy(st[:, :, :, HI0:HI0 + DK], qk4).then_inc(hi_done, 1)
                dve.wait_ge(hi_done, b.after(1, 1))
                for o, slot in ((0, LAST), (H, MID)):
                    v.tensor_tensor(st[:, :, o:o + H, slot:slot + DK], qk4[:, :, o:o + H, :],
                                    st[:, :, o:o + H, HI0:HI0 + DK].bitcast(F32),
                                    ALU.subtract).then_inc(lo_done, 1)

            def route(b):
                dve.wait_ge(route_exp, b.after(1, 1))
                other = ex[:, :, :].unsqueeze(2).to_broadcast([P, NT, E, E])
                own = ex[:, :, :].unsqueeze(3).to_broadcast([P, NT, E, E])
                for t in range(NT):
                    v.tensor_tensor(ge[:, t], other[:, t], own[:, t], ALU.is_ge).then_inc(rank_steps, 1)
                    v.tensor_tensor(gt[:, t], other[:, t], own[:, t], ALU.is_gt).then_inc(rank_steps, 1)
                v.reduce_sum(esum[:, :], ex[:, :, :], AX_X).then_inc(rank_steps, 1)
                dve.wait_ge(rank_steps, b.after(11, 4))
                low = lower[:, :, :].unsqueeze(1).to_broadcast([P, NT, E, E])
                upp = upper[:, :, :].unsqueeze(1).to_broadcast([P, NT, E, E])
                v.tensor_tensor(ge_l[:, :, :, :], ge[:, :, :, :], low, ALU.mult).then_inc(rank_steps, 1)
                v.tensor_tensor(gt_u[:, :, :, :], gt[:, :, :, :], upp, ALU.mult).then_inc(rank_steps, 1)
                dve.wait_ge(rank_steps, b.after(11, 7))
                v.tensor_tensor(beats[:, :, :, :], ge_l[:, :, :, :], gt_u[:, :, :, :], ALU.add
                                ).then_inc(rank_steps, 1)
                dve.wait_ge(rank_steps, b.after(11, 8))
                v.reduce_sum(rank[:, :, :], beats[:, :, :, :], AX_X).then_inc(rank_steps, 1)
                dve.wait_ge(rank_steps, b.after(11, 9))
                v.tensor_scalar(sel[:, :, :], rank[:, :, :], 2.0, None, ALU.is_lt).then_inc(rank_steps, 1)
                v.tensor_scalar(sel_b[:, :, :], rank[:, :, :], 2.0, None, ALU.is_lt).then_inc(sel_ready, 1)
                dve.wait_ge(rank_steps, b.after(11, 10))
                v.tensor_tensor(esel[:, :, :], ex[:, :, :], sel[:, :, :], ALU.mult).then_inc(rank_steps, 1)

            def combine_weights(b):
                dve.wait_ge(rank_steps, b.after(11, 11))
                v.reduce_sum(wsum[:, :], esel[:, :, :], AX_X).then_inc(comb_steps, 1)
                dve.wait_ge(comb_steps, b.after(7, 1))
                v.scalar_tensor_tensor(wden[:, :], esum[:, :], 1e-20, wsum[:, :], ALU.mult, ALU.add
                                       ).then_inc(comb_steps, 1)
                dve.wait_ge(comb_steps, b.after(7, 2))
                v.reciprocal(wrec[:, :], wden[:, :]).then_inc(comb_steps, 1)
                dve.wait_ge(counts_ready, b.after(1, 1))
                pos = ps_t[:, 1, 0:NT * E].rearrange("p (t e) -> p t e", t=NT)
                v.scalar_tensor_tensor(ekeep[:, :, :], pos, float(CAP), esel[:, :, :], ALU.is_lt, ALU.mult
                                       ).then_inc(comb_steps, 1)
                v.tensor_tensor(sel_past[:, :], sel_past[:, :], sel_b[:, 0, :], ALU.add).then_inc(comb_steps, 1)
                dve.wait_ge(comb_steps, b.after(7, 5))
                v.tensor_tensor(sel_past[:, :], sel_past[:, :], sel_b[:, 1, :], ALU.add).then_inc(comb_steps, 1)
                v.tensor_tensor(comb[:, :, :], ekeep[:, :, :], wrec[:, :].unsqueeze(2).to_broadcast([P, NT, E]),
                                ALU.mult).then_inc(comb_steps, 1)

            def ffn(b, k):
                if k < NX:
                    dve.wait_ge(th_done, b.after(NX, k + 1))
                    v.scalar_tensor_tensor(silu[k % 2][:, :], th[k % 2][:, :], 1.0, ps_gu[k % 2][:, 0, :],
                                           ALU.add, ALU.mult).then_inc(silu_done, 1)
                    dve.wait_ge(silu_done, b.after(NX, k + 1))
                    if k >= 3:
                        dve.wait_ge(y_ready, b.after(NY, k - 2))
                    elif before(b) is not None:
                        dve.wait_ge(y_ready, b.after(NY, 0))
                    v.scalar_tensor_tensor(hid[k % 2][:, :], silu[k % 2][:, :], 0.5, ps_gu[k % 2][:, 1, :],
                                           ALU.mult, ALU.mult).then_inc(hid_ready, 1)
                if k < NSH:
                    return
                j = k - NSH + 1
                dve.wait_ge(y_ready, b.after(NY, j))
                yt = ps_y[:, 0, :].rearrange("p (t d) -> p t d", t=NT)
                if j == 1:
                    if before(b) is not None:
                        dve.wait_ge(gacc_ready, b.after(1, 0))
                    v.tensor_copy(acc[:, :, :], yt).then_inc(y_used, 1)
                else:
                    dve.wait_ge(y_used, b.after(NY, j - 1))
                    if j == 2:
                        dve.wait_ge(comb_steps, b.after(7, 7))
                    for t in range(NT):
                        ins = v.scalar_tensor_tensor(acc[:, t, :], yt[:, t, :], comb[:, t, j - 2:j - 1],
                                                     acc[:, t, :], ALU.mult, ALU.add)
                    ins.then_inc(y_used, 1)

            first = True

            def with_split(front, mid, tail):
                nonlocal first
                step(front, mid, tail)
                if first:
                    first = False
                    dve.wait_ge(ffn_loaded, 32)
                    v.tensor_copy(wgu_hi[:, :], wgu_sb[:, :]).then_inc(ffn_split, 1)
                    dve.wait_ge(ffn_split, 1)
                    v.tensor_tensor(wgu_lo[:, :], wgu_sb[:, :], wgu_hi[:, :].bitcast(F32),
                                    ALU.subtract).then_inc(ffn_split, 1)

            run_steps(dve, with_split)

        @block.tensor
        def _(pe):
            mm = nc.tensor.matmul
            tr = nc.tensor.transpose
            pe.wait_ge(c_done, 1)
            pe.wait_ge(consts_ready, 7)
            tr(ps_o[:, 0, 0:B], c_silu[:, :], ident[0:B, 0:B]).then_inc(cT_ready, 1)
            pe.wait_ge(cT_copied, 1)
            pe.wait_ge(weights_loaded, 16 * 5)
            for n, j in enumerate((1, 0, 4, 3)):
                mm(ps_o[:, 1, B * n:B * n + B], wmod_sb[:, D * j:D * j + D], cT[:, :], start=True, stop=True)
            for n, j in enumerate((2, 5)):
                ins = mm(ps_o[0:B, 0, D * n:D * n + D], cT[:, :], wmod_sb[:, D * j:D * j + D],
                         start=True, stop=True)
            ins.then_inc(mod_ready, 1)
            pe.wait_ge(mod_stored, 1)
            pe.wait_ge(dve_consts, 11)

            def step(front, mid, tail):
                for stage, k in STEP:
                    if not has(stage, front, mid, tail):
                        continue
                    if stage == "ln1":
                        b = front
                        if before(b) is not None:
                            pe.wait_ge(q2_copied, b.after(2, 0))
                        pe.wait_ge(xn1_ready, b.after(NT, NT))
                        for t in range(NT):
                            ins = tr(ps_t[:, 0, t * P:t * P + P], xn1[:, t, :], ident[:, :])
                        ins.then_inc(xT1_ready, 1)
                    if stage == "qkv":
                        b = front
                        pe.wait_ge(h1_copied, b.after(1, 1))
                        for t in range(NT):
                            ins = mm(ps_t[:, t, 0:3 * D], h1T[:, t * P:t * P + P], wqkv_sb[:, :],
                                     start=True, stop=True)
                        ins.then_inc(qkv_ready, 1)
                    if stage == "stack":
                        b = front
                        pe.wait_ge(lo_done, b.after(2, 2))
                        pe.wait_ge(hi_again, b.after(2, 2))
                        pe.wait_ge(qkv_read, b.after(5, 5))
                        for f in range(4):
                            if f >= 2:
                                pe.wait_ge(st_copied, b.after(4, f - 1))
                            transpose_stack(f, (NA, NA + 2, 0, 2)[f]).then_inc(st_ready, 1)
                    if stage == "shift":
                        b = mid
                        pe.wait_ge(max_lo, b.after(1, 1))
                        if before(b) is not None:
                            pe.wait_ge(comb_steps, before(b).after(7, 7))
                        for f in range(2):
                            transpose_stack(f, 2 * f).then_inc(q2_ready, 1)
                    if stage == "max":
                        max_round(mid, k)
                    if stage == "exp":
                        exp_round(mid, k)
                    if stage == "wo":
                        b = tail
                        pe.wait_ge(on_ready, b.after(1, 1))
                        if before(b, -1) is not None and mid is not None:
                            pe.wait_ge(st_copied, mid.after(4, 4))
                        for t in range(NT):
                            for j in range(2):
                                ins = mm(ps_t[:, 0, t * P:t * P + P], onT[:, j, t * P:t * P + P],
                                         wo_sb[:, j, :], start=j == 0, stop=j == 1)
                        ins.then_inc(wo_ready, 1)
                    if stage == "ln2":
                        b = tail
                        pe.wait_ge(xn2_ready, b.after(NT, NT))
                        for t in range(NT):
                            ins = tr(ps_t[:, 1, t * P:t * P + P], xn2[:, t, :], ident[:, :])
                        ins.then_inc(xT2_ready, 1)
                    if stage == "logits":
                        b = tail
                        pe.wait_ge(h2_copied, b.after(1, 1))
                        pe.wait_ge(gated_ready, b.after(1, 1))
                        for t in range(NT):
                            ins = mm(ps_t[:, 0, t * E:t * E + E], h2T[:, t * P:t * P + P], gw_sb[:, :],
                                     start=True, stop=True)
                        ins.then_inc(logits_ready, 1)
                    if stage == "counts":
                        b = tail
                        pe.wait_ge(sel_ready, b.after(1, 1))
                        pe.wait_ge(h2_hi_done, b.after(1, 1))
                        if before(b) is not None:
                            pe.wait_ge(comb_steps, b.after(7, 0))
                        at = ps_t[:, 1, :]
                        mm(at[:, 0:E], before_b[:, :], sel_b[:, 0, :], start=True, stop=False)
                        mm(at[:, 0:E], ones_b[:, :], sel_past[:, :], start=False, stop=True)
                        mm(at[:, E:2 * E], before_b[:, :], sel_b[:, 1, :], start=True, stop=False)
                        mm(at[:, E:2 * E], ones_b[:, :], sel_b[:, 0, :], start=False, stop=False)
                        mm(at[:, E:2 * E], ones_b[:, :], sel_past[:, :], start=False, stop=True
                           ).then_inc(counts_ready, 1)
                    if stage == "ffn":
                        ffn(tail, k)

            def transpose_stack(f, block):
                for n in range(2):
                    for t in range(NT):
                        at = n * S + t * P
                        ins = tr(ps_t[:, f % 2, at:at + P],
                                 stack[:, t, (block + n) * P:(block + n + 1) * P].bitcast(F32), ident[:, :])
                return ins

            def max_round(b, r):
                g, blocks, t = score_round(r, True)
                bank = ps_score[r % 2]
                if r >= 2:
                    pe.wait_ge(max_taken, b.after(NR, r - 1))
                elif before(b) is not None:
                    pe.wait_ge(exp_done, b.after(NR, r - 1))
                if r == 0:
                    pe.wait_ge(st_copied, b.after(4, 4))
                n, w = len(blocks), 512 // len(blocks)
                view = bank[:, :].rearrange("p (a q) -> p a q", a=n)
                mm(view[:, :, w - P:w], ident_b[:, :], mask_q[:, 0:n * P].rearrange("p (a q) -> p a q", a=n),
                   start=True, stop=False, skip_group_check=True)
                rows = slice(W * g, W * g + KS)
                for m, a in enumerate(blocks):
                    ins = mm(view[:, m, :], qT[b.p][rows, a, t * P:t * P + P], kT[b.p][rows, a, 0:w],
                             start=False, stop=m == n - 1, skip_group_check=True)
                ins.then_inc(max_scores, 1)

            def exp_round(b, r):
                g, blocks, t = score_round(r, False)
                if r == 0:
                    pe.wait_ge(q2_copied, b.after(2, 2))
                if r >= 2:
                    pe.wait_ge(exp_done, b.after(NR, r - 1))
                else:
                    pe.wait_ge(max_taken, b.after(NR, NR - 1 + r))
                n, w = len(blocks), 512 // len(blocks)
                view = ps_score[r % 2][:, :].rearrange("p (a q) -> p a q", a=n)
                mm(view[:, :, 0:P], ident_b[:, :], mask_k[:, 0:n * P].rearrange("p (a q) -> p a q", a=n),
                   start=True, stop=False, skip_group_check=True)
                rows = slice(W * g, W * g + KM)
                for m, a in enumerate(blocks):
                    ins = mm(view[:, m, :], kT[b.p][rows, a, t * P:t * P + P], qT[b.p][rows, a, S - w:S],
                             start=False, stop=m == n - 1, skip_group_check=True)
                ins.then_inc(exp_scores, 1)
                if r >= 2:
                    values(b, r - 2)
                if r == NR - 1:
                    values(b, r - 1)
                    values(b, r)

            def values(b, r):
                g, blocks, t = score_round(r, False)
                pe.wait_ge(exp_done, b.after(NR, r + 1))
                if r == 0 and before(b) is not None:
                    pe.wait_ge(on_ready, b.after(1, 0))
                n, w = len(blocks), 512 // len(blocks)
                for m, a in enumerate(blocks):
                    ins = mm(ps_o[W * a:W * a + W, g // 2, S - w:S], v_ones[b.p][:, t, 4 * a + g, :],
                             probs[r % NP][:, m * w:m * w + w], start=r < 2, stop=r == NR - 1,
                             skip_group_check=True)
                ins.then_inc(pv_done, 1)

            def ffn(b, k):
                if k < NX:
                    if k == 0:
                        pe.wait_ge(h2_lo_done, b.after(1, 1))
                        if isinstance(b.i, int) and b.index == 0:
                            pe.wait_ge(ffn_split, 2)
                    if k >= 2 or before(b) is not None:
                        pe.wait_ge(hid_ready, b.after(NX, k - 1))
                    for o in range(2):
                        c0 = (2 * k + o) * I
                        at = ps_gu[k % 2][:, o, :]
                        mm(at, wgu_hi[:, c0:c0 + I], h2_hi[:, :], start=True, stop=False)
                        mm(at, wgu_hi[:, c0:c0 + I], h2_lo[:, :], start=False, stop=False)
                        ins = mm(at, wgu_lo[:, c0:c0 + I], h2_hi[:, :], start=False, stop=True)
                    ins.then_inc(gu_ready, 1)
                if k == 0:
                    return
                n = k - 1
                pe.wait_ge(hid_ready, b.after(NX, k))
                if n >= NSH or (n == 0 and before(b) is not None):
                    pe.wait_ge(y_used, b.after(NY, max(n - 1, 0)))
                for t in range(NT):
                    ins = mm(ps_y[:, 0, t * D:t * D + D], hid[n % 2][:, t * P:t * P + P],
                             wd_sb[:, n * D:n * D + D], start=n >= NSH or (n == 0 and t == 0),
                             stop=n >= NSH - 1, skip_group_check=True)
                if n >= NSH - 1:
                    ins.then_inc(y_ready, 1)

            run_steps(pe, step)


def kernel(L0_attn_x, L0_attn_Wq, L0_attn_Wk, L0_attn_Wv, L0_attn_Wo, L0_ffn_gate_w, L0_ffn_we_gate,
           L0_ffn_we_up, L0_ffn_we_down, L0_ffn_ws_gate, L0_ffn_ws_up, L0_ffn_ws_down, L0_c, L0_wmod):
    import concourse.bacc as bacc
    from concourse.bass_utils import run_bass_kernel_spmd

    arr = lambda a: np.asarray(a)
    inv_freq = (np.float32(1.0) / np.float32(10000.0) ** (np.arange(0, DK, 2, dtype=np.float32) / np.float32(DK)))
    theta = np.arange(S, dtype=np.float32)[:, None] * inv_freq[None, :].astype(np.float32)
    sign = np.tile(np.array([-1.0, 1.0], np.float32), DK // 2)
    rope = np.stack([np.repeat(np.cos(theta), 2, axis=-1), np.repeat(np.sin(theta), 2, axis=-1) * sign],
                    axis=1).astype(np.float32)
    wo5 = arr(L0_attn_Wo).reshape(NA, 2, 2, DK, D)
    wo = np.zeros((2, NA, 2, 2 * DK, D), np.float32)
    wo[:, :, :, 0:DK, :] = wo5.transpose(1, 0, 2, 3, 4)
    g = np.concatenate([arr(L0_ffn_ws_gate).reshape(NSH, I, D), arr(L0_ffn_we_gate)])
    u = np.concatenate([arr(L0_ffn_ws_up).reshape(NSH, I, D), arr(L0_ffn_we_up)])
    wgu = np.stack([g, u], axis=1).transpose(3, 0, 1, 2).reshape(D, NX * 2 * I)
    d = np.concatenate([arr(L0_ffn_ws_down).reshape(D, NSH, I).transpose(1, 0, 2), arr(L0_ffn_we_down)])
    wd = d.transpose(2, 0, 1).reshape(I, NX * D)
    arrays = {
        "x": arr(L0_attn_x), "wqkv": np.concatenate([arr(L0_attn_Wq), arr(L0_attn_Wk), arr(L0_attn_Wv)], axis=1),
        "wo": wo.reshape(2, P, D), "gate_w": arr(L0_ffn_gate_w).T, "wgu": wgu, "wd": wd,
        "c": arr(L0_c), "wmod": arr(L0_wmod), "rope": rope,
    }
    nc = bacc.Bacc("TRN2", target_bir_lowering=False, num_devices=1)
    arrays = {f"in_{k}": np.ascontiguousarray(a) for k, a in arrays.items()}
    ins = [nc.dram_tensor(k, a.shape, F32, kind="ExternalInput").ap() for k, a in arrays.items()]
    out = nc.dram_tensor("out_0", (B, S, D), F32, kind="ExternalOutput").ap()
    block_kernel(nc, *ins, out)
    return run_bass_kernel_spmd(nc, [arrays], core_ids=[0]).results[0]["out_0"]
```

```python
from contextlib import ExitStack

import numpy as np

import concourse.bass as bass
from concourse import mybir

F32 = mybir.dt.float32
F32R = mybir.dt.float32r
BF16 = mybir.dt.bfloat16
ALU = mybir.AluOpType
ACT = mybir.ActivationFunctionType
AX_X = mybir.AxisListType.X

P = 128
B, S, D = 16, 256, 128
NT = S // P
H, DK = 16, 8
NA, NG = 4, 4
E, I = 8, 128
NSH = 2
NX = NSH + E
CAP = -(-5 * B * S * 2 // (4 * E))
W = 32
HI0, MID, LAST, MAXC = 0, DK, 2 * DK, 3 * DK
KS = 3 * DK
KM = KS + 2
NR = 12
NP = 4
NH = 4
EPS = 1e-5
NEG = -1e30
SCALE = float(DK) ** -0.5


class Batch:

    def __init__(self, i, c):
        self.i, self.c, self.p = i, c, c % 2

    def shift(self, n):
        return Batch(self.i, self.c + n)

    @property
    def index(self):
        return self.i * 2 + self.c

    def after(self, n, k):
        return self.i * (2 * n) + (n * self.c + k)

    def nth_of_parity(self, n, k):
        return self.i * n + (n * (self.c // 2) + k)


PARTS = {"front": 1, "mid": 0, "tail": -1, "ffn": -2}


ORDER = {
    "pe": """
        mid.max.0 mid.max.1 tail.o_turn ffn.gate_up.0 mid.max.2 tail.on_turn mid.max.3 tail.wo mid.max.4
        ffn.gate_up.1 ffn.gate_up.2 mid.max.5 mid.max.6 ffn.down.0 mid.max.7 mid.max.8 ffn.gate_up.3
        mid.max.9 tail.x2_turn mid.max.10 mid.max.11 ffn.down.1 tail.logits ffn.gate_up.4 ffn.down.2
        mid.shift ffn.gate_up.5 mid.exp.0 mid.exp.1 ffn.down.3 ffn.gate_up.6 mid.exp.2 mid.exp.3 tail.counts
        ffn.down.4 front.x1_turn mid.values.0 mid.exp.4 mid.exp.5 mid.values.1 front.qkv mid.values.2
        ffn.gate_up.7 mid.exp.6 mid.exp.7 mid.values.3 ffn.gate_up.8 mid.values.4 mid.values.5 mid.exp.8
        ffn.down.5 mid.values.6 mid.exp.9 mid.exp.10 ffn.gate_up.9 mid.exp.11 mid.values.7 ffn.down.6
        front.stack.0 front.stack.1 ffn.down.7 mid.values.8 front.stack.2 ffn.down.8 front.stack.3
        mid.values.9 mid.values.10 ffn.down.9 mid.values.11""",
    "act": """
        tail.o_copy ffn.tanh.0 tail.on_copy ffn.tanh.1 ffn.tanh.2 tail.h2 ffn.tanh.3 tail.route ffn.tanh.4
        mid.shift mid.exp.0 mid.exp.1 ffn.tanh.5 ffn.tanh.6 mid.exp.2 mid.exp.3 front.h1 mid.exp.4 mid.exp.5
        ffn.tanh.7 mid.exp.6 mid.exp.7 ffn.tanh.8 mid.exp.8 mid.exp.9 mid.exp.10 ffn.tanh.9 mid.exp.11
        front.stack.0 front.stack.1 front.stack.2 front.stack.3""",
    "dve": """
        mid.max.0 mid.max.1 tail.norm ffn.hidden.0 mid.max.2 mid.max.3 tail.residual mid.max.4 mid.max.5
        ffn.hidden.1 mid.max.6 mid.max.7 tail.normalise mid.max.8 mid.max.9 ffn.hidden.2 mid.max.10
        mid.max.11 tail.logits mid.shift ffn.hidden.3 ffn.hidden.4 front.stats tail.route front.normalise
        tail.comb ffn.hidden.5 ffn.hidden.6 front.rope front.split ffn.hidden.7 ffn.hidden.8 ffn.hidden.9
        ffn.final""",
    "pool": """
        tail.rstd ffn.weigh.2 ffn.weigh.3 ffn.weigh.4 front.rstd mid.mask.0 mid.mask.1 mid.mask.2 mid.mask.3
        ffn.weigh.5 mid.mask.4 mid.mask.5 ffn.weigh.6 mid.mask.6 mid.mask.7 front.again ffn.weigh.7
        mid.mask.8 ffn.weigh.8 mid.mask.9 mid.mask.10 ffn.weigh.9 mid.mask.11""",
    "sp": """
        front.load_x tail.spread mid.load_gates ffn.store""",
}


def stages_of(order):
    parsed = [word.split(".") for word in order.split()]
    return [(w[0], w[1], int(w[2]) if len(w) > 2 else 0) for w in parsed]


PLAN = {name: stages_of(order) for name, order in ORDER.items()}


def run_steps(eng, name, stages, after_first=None):
    def step(batch_of):
        for part, stage, k in PLAN[name]:
            b = batch_of(PARTS[part])
            if b is not None:
                stages[part, stage](b, k)

    def numbered(s):
        return lambda n: Batch((s + n) // 2, (s + n) % 2) if 0 <= s + n < B else None

    first, end = 4, B - 2
    for s in range(-1, first):
        step(numbered(s))
        if s == -1 and after_first is not None:
            after_first()
    with eng.Fori(0, (end - first) // 2) as i:
        for c in range(first, first + 2):
            step(lambda n: Batch(i, c + n))
    for s in range(end, B + 2):
        step(numbered(s))


def before(b, n=1):
    if isinstance(b.i, int) and 2 * b.i + b.c < n:
        return None
    return b.shift(-n)


def score_round(r, first):
    if first:
        return (r, range(NA), 0) if r < 4 else ((r - 4) // 2, range(2 * (r % 2), 2 * (r % 2) + 2), 1)
    return (r // 2, range(2 * (r % 2), 2 * (r % 2) + 2), 0) if r < 8 else (r - 8, range(NA), 1)


def score_shape(r, first):
    n = len(score_round(r, first)[1])
    return n, 512 // n


def block_kernel(nc, x, wqkv, wo, gate_w, wgu, wd, c, wmod, rope, out):
    gate_rows = nc.dram_tensor("gate_rows", [B, 2 * D], F32, kind="Internal").ap()
    comb_rows = nc.dram_tensor("comb_rows", [B, S * E], F32, kind="Internal").ap()
    with ExitStack() as ctx:
        def sb(name, shape, dt=F32):
            return ctx.enter_context(nc.sbuf_tensor(name, shape, dt))

        def sem(name):
            return ctx.enter_context(nc.semaphore(name))

        ps_score = [ctx.enter_context(nc.psum_tensor(f"ps_score{n}", [P, 512], F32)) for n in range(2)]
        ps_gu = [ctx.enter_context(nc.psum_tensor(f"ps_gu{n}", [P, 2, S], F32)) for n in range(2)]
        ps_y = ctx.enter_context(nc.psum_tensor("ps_y", [P, 2, NT * D], F32))
        ps_t = ctx.enter_context(nc.psum_tensor("ps_t", [P, 2, 512], F32))
        ps_o = ctx.enter_context(nc.psum_tensor("ps_o", [P, 2, S], F32))

        wqkv_sb = sb("wqkv_sb", [P, 3 * D])
        wo_sb = sb("wo_sb", [P, D])
        gw_sb = sb("gw_sb", [P, E])
        wgu_sb = sb("wgu_sb", [P, NX * 2 * I])
        wgu_hi = sb("wgu_hi", [P, NX * 2 * I], F32R)
        wgu_lo = sb("wgu_lo", [P, NX * 2 * I], F32R)
        wd_sb = sb("wd_sb", [P, NX * D])
        wmod_sb = sb("wmod_sb", [P, 6 * D])
        rope_sb = sb("rope_sb", [P, NT, 2, DK])
        ident = sb("ident", [P, P])
        ident_b = sb("ident_b", [P, P], BF16)
        mask_q = sb("mask_q", [P, NA * P], BF16)
        before_b = sb("before_b", [P, P], BF16)
        ones_b = sb("ones_b", [P, P], BF16)
        lower = sb("lower", [P, E, E])
        upper = sb("upper", [P, E, E])
        minus_half = sb("minus_half", [P, NT])
        c_sb = sb("c_sb", [B, D])
        c_th = sb("c_th", [B, D])
        c_silu = sb("c_silu", [B, D])
        cT = sb("cT", [P, B])
        mod = sb("mod", [P, B, 4])
        gate_raw = sb("gate_raw", [B, 2 * D])
        gate_sign = sb("gate_sign", [B, 2 * D])
        gate_mag = sb("gate_mag", [B, 2 * D])
        x_sb = [sb(f"x_sb{n}", [P, NT, D]) for n in range(2)]
        gates = [sb(f"gates{n}", [P, 2 * D]) for n in range(2)]
        st1 = sb("st1", [P, NT, 6])
        mv1 = sb("mv1", [P, NT, 2])
        ve1 = sb("ve1", [P, NT])
        rstd1 = sb("rstd1", [P, NT])
        xn1 = sb("xn1", [P, NT, D])
        h1T = sb("h1T", [P, S])
        qk_cos = sb("qk_cos", [P, NT, 2 * D])
        qk_sin = sb("qk_sin", [P, NT, 2 * D])
        qk = sb("qk", [P, NT, 2 * D])
        stack = sb("stack", [P, NT, 2 * H * W], F32R)
        v_ones = [sb(f"v_ones{n}", [P, NT, H, W]) for n in range(2)]
        qT = [sb(f"qT{n}", [P, NA, S], F32R) for n in range(2)]
        kT = [sb(f"kT{n}", [P, NA, S], F32R) for n in range(2)]
        mx = sb("mx", [P, NT, H])
        probs = [sb(f"probs{n}", [P, 512]) for n in range(NP)]
        oT = sb("oT", [P, 2, S])
        rden = sb("rden", [P, NT * H])
        on = sb("on", [P, NT * H, DK])
        onT = sb("onT", [P, S])
        gated = sb("gated", [P, NT, D])
        x1 = [sb(f"x1_{n}", [P, NT, D]) for n in range(2)]
        st2 = sb("st2", [P, NT, 6])
        mv2 = sb("mv2", [P, NT, 2])
        ve2 = sb("ve2", [P, NT])
        rstd2 = sb("rstd2", [P, NT])
        xn2 = sb("xn2", [P, NT, D])
        h2T = sb("h2T", [P, S])
        h2_hi = [sb(f"h2_hi{n}", [P, S], F32R) for n in range(2)]
        h2_lo = [sb(f"h2_lo{n}", [P, S], F32R) for n in range(2)]
        lmax = sb("lmax", [P, NT])
        ldif = sb("ldif", [P, NT, E])
        ex = sb("ex", [P, NT, E])
        ge = sb("ge", [P, NT, E, E])
        gt = sb("gt", [P, NT, E, E])
        ge_l = sb("ge_l", [P, NT, E, E])
        gt_u = sb("gt_u", [P, NT, E, E])
        beats = sb("beats", [P, NT, E, E])
        rank = sb("rank", [P, NT, E])
        sel = sb("sel", [P, NT, E])
        sel_b = sb("sel_b", [P, NT, E], BF16)
        sel_past = sb("sel_past", [P, E], BF16)
        esum = sb("esum", [P, NT])
        esel = sb("esel", [P, NT, E])
        wsum = sb("wsum", [P, NT])
        wden = sb("wden", [P, NT])
        wrec = sb("wrec", [P, NT])
        ekeep = sb("ekeep", [P, NT, E])
        comb = [sb(f"comb{n}", [P, NT, E]) for n in range(2)]
        th = [sb(f"th{n}", [P, S]) for n in range(2)]
        silu = [sb(f"silu{n}", [P, S]) for n in range(2)]
        hid = [sb(f"hid{n}", [P, S]) for n in range(NH)]
        comb_all = [sb(f"comb_all{n}", [P, S * E]) for n in range(2)]
        gacc = sb("gacc", [P, NT, D])
        out_sb = [sb(f"out_sb{n}", [P, NT, D]) for n in range(2)]

        passed = sem("passed")
        c_loaded, weights_loaded, ffn_loaded = sem("c_loaded"), sem("weights_loaded"), sem("ffn_loaded")
        c_tanh, c_done, cT_ready, cT_copied, mod_ready, mod_stored = (
            sem("c_tanh"), sem("c_done"), sem("cT_ready"), sem("cT_copied"), sem("mod_ready"), sem("mod_stored"))
        setup_pool, setup_dve, gates_computed, gates_written = (
            sem("setup_pool"), sem("setup_dve"), sem("gates_computed"), sem("gates_written"))
        consts_ready, dve_consts, ffn_split = sem("consts_ready"), sem("dve_consts"), sem("ffn_split")
        x_loaded = [sem(f"x_loaded{n}") for n in range(2)]
        gates_loaded = [sem(f"gates_loaded{n}") for n in range(2)]
        ln1_stats, ln1_mv, ln1_var, ln1_rstd, xn1_ready = (
            sem("ln1_stats"), sem("ln1_mv"), sem("ln1_var"), sem("ln1_rstd"), sem("xn1_ready"))
        xT1_ready, h1_copied, qkv_ready = sem("xT1_ready"), sem("h1_copied"), sem("qkv_ready")
        qkv_read, rope_done, hi_done, lo_done, hi_again = (
            sem("qkv_read"), sem("rope_done"), sem("hi_done"), sem("lo_done"), sem("hi_again"))
        st_ready, st_copied = sem("st_ready"), sem("st_copied")
        max_scores, max_taken = sem("max_scores"), sem("max_taken")
        max_hi, max_lo, q2_ready, q2_copied = sem("max_hi"), sem("max_lo"), sem("q2_ready"), sem("q2_copied")
        exp_scores, exp_done, pv_done = sem("exp_scores"), sem("exp_done"), sem("pv_done")
        exp_masked = sem("exp_masked")
        o_copied, o_turned, den_rec, on_ready, on_turned, on_copied = (
            sem("o_copied"), sem("o_turned"), sem("den_rec"), sem("on_ready"), sem("on_turned"), sem("on_copied"))
        wo_ready, gated_ready, x1_ready = sem("wo_ready"), sem("gated_ready"), sem("x1_ready")
        ln2_stats, ln2_mv, ln2_var, ln2_rstd, xn2_ready = (
            sem("ln2_stats"), sem("ln2_mv"), sem("ln2_var"), sem("ln2_rstd"), sem("xn2_ready"))
        xT2_ready, h2_copied, h2_hi_done, h2_lo_done = (
            sem("xT2_ready"), sem("h2_copied"), sem("h2_hi_done"), sem("h2_lo_done"))
        logits_ready, lmax_done, ldif_done, route_exp = (
            sem("logits_ready"), sem("lmax_done"), sem("ldif_done"), sem("route_exp"))
        rank_steps, sel_ready, counts_ready, comb_steps = (
            sem("rank_steps"), sem("sel_ready"), sem("counts_ready"), sem("comb_steps"))
        gu_ready, th_done, silu_done, hid_ready = (
            sem("gu_ready"), sem("th_done"), sem("silu_done"), sem("hid_ready"))
        hid_weighed, down_done = sem("hid_weighed"), sem("down_done")
        comb_stored, comb_spread = ([sem(f"{n}{p}") for p in range(2)] for n in ("comb_stored", "comb_spread"))
        gacc_ready, out_ready = sem("gacc_ready"), sem("out_ready")
        out_stored = [sem(f"out_stored{n}") for n in range(2)]

        heads = lambda t: t.rearrange("p t (h w) -> p t h w", w=W)

        def hid_of(b, k):
            return (NX % NH * b.p + k) % NH

        SETUP_LOADS = 6

        block = ctx.enter_context(nc.Block())

        def wait_apart(eng, signal, value):
            eng.wait_ge(signal, value)
            eng.sem_inc(passed, 1)

        @block.sync
        def _(sp):
            sp.dma_start(c_sb[:, :], c).then_inc(c_loaded, 16)
            for dst, src in ((wmod_sb[:, :], wmod), (wqkv_sb[:, :], wqkv),
                             (rope_sb[:, :, :, :], rope.rearrange("(t p) a d -> p t a d", p=P)),
                             (wo_sb[:, :], wo), (gw_sb[:, :], gate_w)):
                sp.dma_start(dst, src).then_inc(weights_loaded, 16)

            def feed_forward_weights():
                sp.dma_start(wgu_sb[:, :], wgu).then_inc(ffn_loaded, 16)
                sp.dma_start(wd_sb[:, :], wd).then_inc(ffn_loaded, 16)
                sp.wait_ge(gates_computed, 1)
                sp.dma_start(gate_rows, gate_mag[:, :]).then_inc(gates_written, 16)
                sp.wait_ge(gates_written, 16)

            def load_x(b, _):
                old = before(b, 2)
                if old is not None:
                    sp.wait_ge(x1_ready, old.after(1, 1))
                sp.dma_start(x_sb[b.p][:, :, :],
                             x[bass.ds(b.index, 1)].rearrange("o (t p) d -> p (o t) d", p=P)
                             ).then_inc(x_loaded[b.p], 16)

            def load_gates(b, _):
                old = before(b, 2)
                if old is not None:
                    sp.wait_ge(out_ready, old.after(1, 1))
                sp.dma_start(gates[b.p][:, :], gate_rows[bass.ds(b.index, 1)].to_broadcast([P, 2 * D])
                             ).then_inc(gates_loaded[b.p], 16)

            def spread(b, _):
                wait_apart(sp, comb_steps, b.after(7, 7))
                sp.dma_start(comb_rows[bass.ds(b.index, 1)].rearrange("o (p c) -> p (o c)", p=P),
                             comb[b.p][:, :, :].rearrange("p t e -> p (t e)")).then_inc(comb_stored[b.p], 16)
                wait_apart(sp, comb_stored[b.p], b.nth_of_parity(16, 16))
                old = before(b, 2)
                if old is not None:
                    wait_apart(sp, hid_weighed, old.after(E, E))
                sp.dma_start(comb_all[b.p][:, :], comb_rows[bass.ds(b.index, 1)].to_broadcast([P, S * E])
                             ).then_inc(comb_spread[b.p], 16)

            def store(b, _):
                sp.wait_ge(out_ready, b.after(1, 1))
                sp.dma_start(out[bass.ds(b.index, 1)].rearrange("o (t p) d -> p (o t) d", p=P),
                             out_sb[b.p][:, :, :]).then_inc(out_stored[b.p], 16)

            run_steps(sp, "sp", {("front", "load_x"): load_x, ("mid", "load_gates"): load_gates,
                                 ("tail", "spread"): spread, ("ffn", "store"): store}, feed_forward_weights)
            for n in range(2):
                sp.wait_ge(out_stored[n], 16 * (B // 2))

        @block.gpsimd
        def _(pool):
            n = 0

            def link(ins):
                nonlocal n
                n += 1
                ins.then_inc(setup_pool, 1)
                pool.wait_ge(setup_pool, n)

            g = nc.gpsimd
            link(g.memset(ident[:, :], 0.0))
            link(g.affine_select(out=ident[:, :], in_=ident[:, :], compare_op=ALU.not_equal, fill=1.0,
                                 base=0, pattern=[[-1, P]], channel_multiplier=1))
            g.tensor_copy(ident_b[:, :], ident[:, :]).then_inc(consts_ready, 1)
            g.memset(minus_half[:, :], -0.5).then_inc(consts_ready, 1)
            link(g.memset(mask_q[:, :], 0.0))
            g.affine_select(out=mask_q[:, :], in_=mask_q[:, :], compare_op=ALU.is_ge, fill=NEG, base=0,
                            pattern=[[0, NA], [-1, P]], channel_multiplier=1).then_inc(consts_ready, 1)
            link(g.memset(before_b[:, :], 1.0))
            g.affine_select(out=before_b[:, :], in_=before_b[:, :], compare_op=ALU.is_gt, fill=0.0, base=0,
                            pattern=[[1, P]], channel_multiplier=-1).then_inc(consts_ready, 1)
            link(g.memset(lower[:, :, :], 1.0))
            g.affine_select(out=lower[:, :, :], in_=lower[:, :, :], compare_op=ALU.is_gt, fill=0.0, base=0,
                            pattern=[[1, E], [-1, E]], channel_multiplier=0).then_inc(consts_ready, 1)
            link(g.memset(upper[:, :, :], 1.0))
            g.affine_select(out=upper[:, :, :], in_=upper[:, :, :], compare_op=ALU.is_gt, fill=0.0, base=0,
                            pattern=[[-1, E], [1, E]], channel_multiplier=0).then_inc(consts_ready, 1)

            def rstd1_of(b, _):
                wait_apart(pool, ln1_mv, b.after(1, 1))
                g.tensor_scalar(ve1[:, :], mv1[:, :, 1], EPS, None, ALU.add).then_inc(ln1_var, 1)
                pool.wait_ge(ln1_var, b.after(1, 1))
                g.tensor_tensor(rstd1[:, :], ve1[:, :], minus_half[:, :], ALU.pow).then_inc(ln1_rstd, 1)

            def rstd2_of(b, _):
                wait_apart(pool, ln2_mv, b.after(1, 1))
                g.tensor_scalar(ve2[:, :], mv2[:, :, 1], EPS, None, ALU.add).then_inc(ln2_var, 1)
                pool.wait_ge(ln2_var, b.after(1, 1))
                g.tensor_tensor(rstd2[:, :], ve2[:, :], minus_half[:, :], ALU.pow).then_inc(ln2_rstd, 1)

            def again(b, _):
                wait_apart(pool, hi_done, b.after(1, 1))
                st = heads(stack[:, :, :])
                for o, slot in ((0, MID), (H, LAST)):
                    g.tensor_copy(st[:, :, o:o + H, slot:slot + DK].bitcast(F32),
                                  st[:, :, o:o + H, HI0:HI0 + DK].bitcast(F32)).then_inc(hi_again, 1)

            def mask(b, r):
                n, w = score_shape(r, False)
                wait_apart(pool, exp_done, b.after(NR, r + 1))
                v = probs[r % NP][:, :].rearrange("p (a q) -> p a q", a=n)[:, :, 0:P]
                g.affine_select(out=v, in_=v, compare_op=ALU.is_ge, fill=0.0, base=0,
                                pattern=[[0, n], [1, P]], channel_multiplier=-1).then_inc(exp_masked, 1)

            def weigh(b, k):
                if k == NSH:
                    pool.wait_ge(comb_spread[b.p], b.nth_of_parity(16, 16))
                pool.wait_ge(hid_ready, b.after(NX, k + 1))
                h = hid[hid_of(b, k)][:, :].rearrange("i (t p) -> i t p", t=NT)
                w = comb_all[b.p][:, :].rearrange("i (p t e) -> i e t p", t=NT, e=E)[:, k - NSH]
                g.tensor_tensor(h, h, w, ALU.mult).then_inc(hid_weighed, 1)

            run_steps(pool, "pool", {("ffn", "weigh"): weigh,
                                     ("front", "rstd"): rstd1_of, ("tail", "rstd"): rstd2_of,
                                     ("front", "again"): again, ("mid", "mask"): mask})

        @block.scalar
        def _(act):
            s = nc.scalar
            act.wait_ge(c_loaded, 16)
            s.activation(c_th[:, :], c_sb[:, :], ACT.Tanh, scale=0.5).then_inc(c_tanh, 1)

            def transposed(dst, src, b, which):
                m = mod[:, bass.ds(b.index, 1), :]
                return s.activation(dst, src, ACT.Identity,
                                    scale=m[:, :, which:which + 1].rearrange("p o k -> p (o k)"),
                                    bias=m[:, :, which + 1:which + 2].rearrange("p o k -> p (o k)"))

            def h1(b, _):
                if isinstance(b.i, int) and b.index == 0:
                    act.wait_ge(mod_stored, 1)
                act.wait_ge(xT1_ready, b.after(1, 1))
                transposed(h1T[:, :], ps_t[:, 0, 0:S], b, 0).then_inc(h1_copied, 1)

            def stack_copy(b, f):
                act.wait_ge(st_ready, b.after(4, f + 1))
                dst = (kT, kT, qT, qT)[f][b.p][:, 2 * (f % 2):2 * (f % 2) + 2, :]
                s.activation(dst, ps_t[:, f % 2, :].rearrange("p (a q) -> p a q", a=2),
                             ACT.Copy).then_inc(st_copied, 1)

            def shift(b, _):
                for f in range(2):
                    act.wait_ge(q2_ready, b.after(2, f + 1))
                    s.activation(qT[b.p][:, 2 * f:2 * f + 2, :],
                                 ps_t[:, f, :].rearrange("p (a q) -> p a q", a=2),
                                 ACT.Copy).then_inc(q2_copied, 1)

            def exp(b, r):
                act.wait_ge(exp_scores, b.after(NR, r + 1))
                if r >= NP or before(b) is not None:
                    act.wait_ge(pv_done, b.after(NR, r - NP + 1))
                s.activation(probs[r % NP][:, :], ps_score[r % 2][:, :], ACT.Exp,
                             scale=SCALE).then_inc(exp_done, 1)

            def o_copy(b, _):
                act.wait_ge(pv_done, b.after(NR, NR))
                s.activation(oT[:, :, :], ps_o[:, :, :], ACT.Copy).then_inc(o_copied, 1)

            def on_copy(b, _):
                act.wait_ge(on_turned, b.after(1, 1))
                s.activation(onT[:, :], ps_t[:, 1, 0:S], ACT.Copy).then_inc(on_copied, 1)

            def h2(b, _):
                act.wait_ge(xT2_ready, b.after(1, 1))
                transposed(h2_hi[b.p][:, :], ps_t[:, 1, 0:S], b, 2).then_inc(h2_hi_done, 1)
                transposed(h2T[:, :], ps_t[:, 1, 0:S], b, 2).then_inc(h2_copied, 1)

            def route(b, _):
                act.wait_ge(ldif_done, b.after(1, 1))
                s.activation(ex[:, :, :], ldif[:, :, :], ACT.Exp).then_inc(route_exp, 1)

            def tanh(b, k):
                act.wait_ge(gu_ready, b.after(NX, k + 1))
                s.activation(th[k % 2][:, :], ps_gu[k % 2][:, 0, :], ACT.Tanh, scale=0.5).then_inc(th_done, 1)

            run_steps(act, "act", {
                ("front", "h1"): h1, ("front", "stack"): stack_copy, ("mid", "shift"): shift,
                ("mid", "exp"): exp, ("tail", "o_copy"): o_copy, ("tail", "on_copy"): on_copy,
                ("tail", "h2"): h2, ("tail", "route"): route, ("ffn", "tanh"): tanh})

        @block.vector
        def _(dve):
            v = nc.vector
            n = 0

            def link(ins):
                nonlocal n
                n += 1
                ins.then_inc(setup_dve, 1)
                dve.wait_ge(setup_dve, n)

            dve.wait_ge(c_tanh, 1)
            link(v.tensor_scalar(c_th[:, :], c_th[:, :], 1.0, 0.5, ALU.add, ALU.mult))
            v.tensor_tensor(c_silu[:, :], c_th[:, :], c_sb[:, :], ALU.mult).then_inc(c_done, 1)
            link(v.memset(stack[:, :, :].bitcast(F32), 0.0))
            v.memset(heads(stack[:, :, :])[:, :, H:2 * H, MAXC:MAXC + 2].bitcast(F32), 1.0).then_inc(dve_consts, 1)
            dve.wait_ge(cT_ready, 1)
            v.tensor_copy(cT[:, :], ps_o[:, 0, 0:B]).then_inc(cT_copied, 1)
            dve.wait_ge(mod_ready, 1)
            mv = ps_o[:, 1, 0:4 * B].rearrange("p (k b) -> p b k", b=B)
            link(v.tensor_copy(gate_raw[:, :], ps_o[0:B, 0, 0:2 * D]))
            for k in range(4):
                ins = v.tensor_scalar(mod[:, :, k], mv[:, :, k], 1.0 if k % 2 == 0 else 0.0, None, ALU.add)
                if k < 3:
                    link(ins)
            ins.then_inc(mod_stored, 1)

            def rest_of_setup():
                link(v.tensor_scalar(gate_sign[:, :], gate_raw[:, :], 0.0, 2.0, ALU.is_ge, ALU.mult))
                link(v.tensor_scalar(gate_mag[:, :], gate_raw[:, :], -1.0, None, ALU.mult))
                link(v.tensor_tensor(gate_raw[:, :], gate_mag[:, :], gate_raw[:, :], ALU.max))
                link(v.tensor_scalar(gate_raw[:, :], gate_raw[:, :], 0.25, None, ALU.max))
                v.scalar_tensor_tensor(gate_mag[:, :], gate_sign[:, :], -1.0, gate_raw[:, :],
                                       ALU.add, ALU.mult).then_inc(gates_computed, 1)
                dve.wait_ge(ffn_loaded, 32)
                v.tensor_copy(wgu_hi[:, :], wgu_sb[:, :]).then_inc(ffn_split, 1)
                dve.wait_ge(ffn_split, 1)
                v.tensor_tensor(wgu_lo[:, :], wgu_sb[:, :], wgu_hi[:, :].bitcast(F32),
                                ALU.subtract).then_inc(ffn_split, 1)

            def vone_consts():
                for n2 in range(2):
                    link(v.memset(v_ones[n2][:, :, :, :], 0.0))
                    pair = v_ones[n2][:, :, :, :].rearrange("p t (c o) w -> p t c o w", o=2)
                    for o in range(2):
                        for t in range(NT):
                            v.memset(pair[:, t, :, o, 16 * o + DK:16 * o + 2 * DK], 1.0).then_inc(dve_consts, 1)
                v.memset(ones_b[:, :], 1.0).then_inc(dve_consts, 1)
                v.memset(sel_past[:, :], 0.0).then_inc(dve_consts, 1)

            vone_consts()

            def layer_stats(b, src, st, mv, stats, done):
                for t in range(NT):
                    v.bn_stats(st[:, t, :], src[:, t, :]).then_inc(stats, 1)
                wait_apart(dve, stats, b.after(NT, NT))
                for t in range(NT):
                    ins = v.bn_aggr(mv[:, t, :], st[:, t, :])
                ins.then_inc(done, 1)

            def normalise(b, src, mv, rstd, dst, ready, done):
                dve.wait_ge(ready, b.after(1, 1))
                for t in range(NT):
                    v.tensor_scalar(dst[:, t, :], src[:, t, :], mv[:, t, 0:1], rstd[:, t:t + 1],
                                    ALU.subtract, ALU.mult).then_inc(done, 1)

            def front_stats(b, _):
                dve.wait_ge(x_loaded[b.p], b.nth_of_parity(16, 16))
                layer_stats(b, x_sb[b.p], st1, mv1, ln1_stats, ln1_mv)

            def front_normalise(b, _):
                normalise(b, x_sb[b.p], mv1, rstd1, xn1, ln1_rstd, xn1_ready)

            def rope_turn(b, _):
                raw = ps_t[:, :, 0:2 * D].rearrange("p t (h d) -> p t h d", d=DK)
                cos = rope_sb[:, :, 0, :].unsqueeze(2).to_broadcast([P, NT, 2 * H, DK])
                sin = rope_sb[:, :, 1, :].unsqueeze(2).to_broadcast([P, NT, 2 * H, DK])
                dve.wait_ge(qkv_ready, b.after(1, 1))
                v.tensor_tensor(qk_cos[:, :, :].rearrange("p t (h d) -> p t h d", d=DK), raw, cos,
                                ALU.mult).then_inc(qkv_read, 1)
                sn = qk_sin[:, :, :].rearrange("p t (h d) -> p t h d", d=DK)
                for o in range(2):
                    v.tensor_tensor(sn[:, :, :, o::2], raw[:, :, :, 1 - o::2], sin[:, :, :, o::2],
                                    ALU.mult).then_inc(qkv_read, 1)
                if before(b, 2) is not None:
                    dve.wait_ge(pv_done, before(b, 2).after(NR, NR))
                val = ps_t[:, :, 2 * D:3 * D].rearrange("p t (c o d) -> p t c o d", o=2, d=DK)
                vo = v_ones[b.p][:, :, :, :].rearrange("p t (c o) w -> p t c o w", o=2)
                for o in range(2):
                    v.tensor_copy(vo[:, :, :, o, 16 * o:16 * o + DK], val[:, :, :, o, :]).then_inc(qkv_read, 1)
                dve.wait_ge(qkv_read, b.after(5, 3))
                v.tensor_tensor(qk[:, :, :], qk_cos[:, :, :], qk_sin[:, :, :], ALU.add).then_inc(rope_done, 1)

            def split(b, _):
                st = heads(stack[:, :, :])
                dve.wait_ge(rope_done, b.after(1, 1))
                if before(b) is not None:
                    dve.wait_ge(q2_ready, before(b).after(2, 2))
                qk4 = qk[:, :, :].rearrange("p t (h d) -> p t h d", d=DK)
                v.tensor_copy(st[:, :, :, HI0:HI0 + DK], qk4).then_inc(hi_done, 1)
                dve.wait_ge(hi_done, b.after(1, 1))
                for o, slot in ((0, LAST), (H, MID)):
                    v.tensor_tensor(st[:, :, o:o + H, slot:slot + DK], qk4[:, :, o:o + H, :],
                                    st[:, :, o:o + H, HI0:HI0 + DK].bitcast(F32),
                                    ALU.subtract).then_inc(lo_done, 1)

            def row_max(b, r):
                g, blocks, t = score_round(r, True)
                dve.wait_ge(max_scores, b.after(NR, r + 1))
                v.reduce_max(mx[:, t, :].rearrange("p (a g) -> p a g", g=NG)[:, blocks[0]:blocks[-1] + 1, g],
                             ps_score[r % 2][:, :].rearrange("p (a q) -> p a q", a=len(blocks)),
                             AX_X).then_inc(max_taken, 1)

            def shift(b, _):
                q = heads(stack[:, :, :])[:, :, 0:H, :]
                dve.wait_ge(max_taken, b.after(NR, NR))
                v.tensor_scalar(q[:, :, :, MAXC], mx[:, :, :], -1.0, None, ALU.mult).then_inc(max_hi, 1)
                dve.wait_ge(max_hi, b.after(1, 1))
                v.scalar_tensor_tensor(q[:, :, :, MAXC + 1], mx[:, :, :], -1.0,
                                       q[:, :, :, MAXC].bitcast(F32), ALU.mult,
                                       ALU.subtract).then_inc(max_lo, 1)

            def norm(b, _):
                dve.wait_ge(o_turned, b.after(1, 1))
                o = ps_t[:, 0, :].rearrange("p (c w) -> p c w", w=2 * DK)
                v.reciprocal(rden[:, :], o[:, :, DK]).then_inc(den_rec, 1)
                dve.wait_ge(den_rec, b.after(1, 1))
                v.tensor_tensor(on[:, :, :], o[:, :, 0:DK], rden[:, :].unsqueeze(2).to_broadcast([P, NT * H, DK]),
                                ALU.mult).then_inc(on_ready, 1)

            def residual(b, _):
                dve.wait_ge(gates_loaded[b.p], b.nth_of_parity(16, 16))
                dve.wait_ge(wo_ready, b.after(1, 1))
                ga = gates[b.p][:, 0:D].unsqueeze(1).to_broadcast([P, NT, D])
                v.tensor_tensor(gated[:, :, :], ps_t[:, 0, 0:S].rearrange("p (t d) -> p t d", t=NT),
                                ga, ALU.mult).then_inc(gated_ready, 1)
                dve.wait_ge(gated_ready, b.after(1, 1))
                v.tensor_tensor(x1[b.p][:, :, :], gated[:, :, :], x_sb[b.p][:, :, :], ALU.add
                                ).then_inc(x1_ready, 1)
                dve.wait_ge(x1_ready, b.after(1, 1))
                layer_stats(b, x1[b.p], st2, mv2, ln2_stats, ln2_mv)

            def tail_normalise(b, _):
                normalise(b, x1[b.p], mv2, rstd2, xn2, ln2_rstd, xn2_ready)

            def logits(b, _):
                dve.wait_ge(h2_hi_done, b.after(1, 1))
                dve.wait_ge(h2_copied, b.after(1, 1))
                v.tensor_tensor(h2_lo[b.p][:, :], h2T[:, :], h2_hi[b.p][:, :].bitcast(F32),
                                ALU.subtract).then_inc(h2_lo_done, 1)
                dve.wait_ge(logits_ready, b.after(1, 1))
                lg = ps_t[:, 0, 0:NT * E].rearrange("p (t e) -> p t e", t=NT)
                v.reduce_max(lmax[:, :], lg, AX_X).then_inc(lmax_done, 1)
                dve.wait_ge(lmax_done, b.after(1, 1))
                v.tensor_tensor(ldif[:, :, :], lg, lmax[:, :].unsqueeze(2).to_broadcast([P, NT, E]),
                                ALU.subtract).then_inc(ldif_done, 1)

            def route(b, _):
                dve.wait_ge(route_exp, b.after(1, 1))
                other = ex[:, :, :].unsqueeze(2).to_broadcast([P, NT, E, E])
                own = ex[:, :, :].unsqueeze(3).to_broadcast([P, NT, E, E])
                for t in range(NT):
                    v.tensor_tensor(ge[:, t], other[:, t], own[:, t], ALU.is_ge).then_inc(rank_steps, 1)
                    v.tensor_tensor(gt[:, t], other[:, t], own[:, t], ALU.is_gt).then_inc(rank_steps, 1)
                v.reduce_sum(esum[:, :], ex[:, :, :], AX_X).then_inc(rank_steps, 1)
                dve.wait_ge(rank_steps, b.after(11, 4))
                low = lower[:, :, :].unsqueeze(1).to_broadcast([P, NT, E, E])
                upp = upper[:, :, :].unsqueeze(1).to_broadcast([P, NT, E, E])
                v.tensor_tensor(ge_l[:, :, :, :], ge[:, :, :, :], low, ALU.mult).then_inc(rank_steps, 1)
                v.tensor_tensor(gt_u[:, :, :, :], gt[:, :, :, :], upp, ALU.mult).then_inc(rank_steps, 1)
                dve.wait_ge(rank_steps, b.after(11, 7))
                v.tensor_tensor(beats[:, :, :, :], ge_l[:, :, :, :], gt_u[:, :, :, :], ALU.add
                                ).then_inc(rank_steps, 1)
                dve.wait_ge(rank_steps, b.after(11, 8))
                v.reduce_sum(rank[:, :, :], beats[:, :, :, :], AX_X).then_inc(rank_steps, 1)
                dve.wait_ge(rank_steps, b.after(11, 9))
                v.tensor_scalar(sel[:, :, :], rank[:, :, :], 2.0, None, ALU.is_lt).then_inc(rank_steps, 1)
                v.tensor_scalar(sel_b[:, :, :], rank[:, :, :], 2.0, None, ALU.is_lt).then_inc(sel_ready, 1)
                dve.wait_ge(rank_steps, b.after(11, 10))
                v.tensor_tensor(esel[:, :, :], ex[:, :, :], sel[:, :, :], ALU.mult).then_inc(rank_steps, 1)

            def combine_weights(b, _):
                dve.wait_ge(rank_steps, b.after(11, 11))
                v.reduce_sum(wsum[:, :], esel[:, :, :], AX_X).then_inc(comb_steps, 1)
                dve.wait_ge(comb_steps, b.after(7, 1))
                v.scalar_tensor_tensor(wden[:, :], esum[:, :], 1e-20, wsum[:, :], ALU.mult, ALU.add
                                       ).then_inc(comb_steps, 1)
                dve.wait_ge(comb_steps, b.after(7, 2))
                v.reciprocal(wrec[:, :], wden[:, :]).then_inc(comb_steps, 1)
                dve.wait_ge(counts_ready, b.after(1, 1))
                pos = ps_t[:, 1, 0:NT * E].rearrange("p (t e) -> p t e", t=NT)
                v.scalar_tensor_tensor(ekeep[:, :, :], pos, float(CAP), esel[:, :, :], ALU.is_lt, ALU.mult
                                       ).then_inc(comb_steps, 1)
                v.tensor_tensor(sel_past[:, :], sel_past[:, :], sel_b[:, 0, :], ALU.add).then_inc(comb_steps, 1)
                dve.wait_ge(comb_steps, b.after(7, 5))
                v.tensor_tensor(sel_past[:, :], sel_past[:, :], sel_b[:, 1, :], ALU.add).then_inc(comb_steps, 1)
                v.tensor_tensor(comb[b.p][:, :, :], ekeep[:, :, :],
                                wrec[:, :].unsqueeze(2).to_broadcast([P, NT, E]), ALU.mult).then_inc(comb_steps, 1)

            def hidden(b, k):
                dve.wait_ge(th_done, b.after(NX, k + 1))
                v.scalar_tensor_tensor(silu[k % 2][:, :], th[k % 2][:, :], 1.0, ps_gu[k % 2][:, 0, :],
                                       ALU.add, ALU.mult).then_inc(silu_done, 1)
                dve.wait_ge(silu_done, b.after(NX, k + 1))
                if k >= NH or before(b) is not None:
                    dve.wait_ge(down_done, b.after(NX, k - NH + 1))
                v.scalar_tensor_tensor(hid[hid_of(b, k)][:, :], silu[k % 2][:, :], 0.5, ps_gu[k % 2][:, 1, :],
                                       ALU.mult, ALU.mult).then_inc(hid_ready, 1)

            def final(b, _):
                dve.wait_ge(down_done, b.after(NX, NX))
                gb = gates[b.p][:, D:2 * D].unsqueeze(1).to_broadcast([P, NT, D])
                y = ps_y[:, 0, :].rearrange("p (t d) -> p t d", t=NT)
                v.tensor_tensor(gacc[:, :, :], y, gb, ALU.mult).then_inc(gacc_ready, 1)
                dve.wait_ge(gacc_ready, b.after(1, 1))
                old = before(b, 2)
                if old is not None:
                    dve.wait_ge(out_stored[b.p], old.nth_of_parity(16, 16))
                v.tensor_tensor(out_sb[b.p][:, :, :], gacc[:, :, :], x1[b.p][:, :, :],
                                ALU.add).then_inc(out_ready, 1)

            run_steps(dve, "dve", {
                ("front", "stats"): front_stats, ("front", "normalise"): front_normalise,
                ("front", "rope"): rope_turn, ("front", "split"): split,
                ("mid", "max"): row_max, ("mid", "shift"): shift,
                ("tail", "norm"): norm, ("tail", "residual"): residual, ("tail", "normalise"): tail_normalise,
                ("tail", "logits"): logits, ("tail", "route"): route, ("tail", "comb"): combine_weights,
                ("ffn", "hidden"): hidden, ("ffn", "final"): final}, rest_of_setup)

        @block.tensor
        def _(pe):
            mm = nc.tensor.matmul
            tr = nc.tensor.transpose
            pe.wait_ge(c_done, 1)
            pe.wait_ge(consts_ready, 6)
            tr(ps_o[:, 0, 0:B], c_silu[:, :], ident[0:B, 0:B]).then_inc(cT_ready, 1)
            pe.wait_ge(cT_copied, 1)
            pe.wait_ge(weights_loaded, 16 * 5)
            for n, j in enumerate((1, 0, 4, 3)):
                mm(ps_o[:, 1, B * n:B * n + B], wmod_sb[:, D * j:D * j + D], cT[:, :], start=True, stop=True)
            for n, j in enumerate((2, 5)):
                ins = mm(ps_o[0:B, 0, D * n:D * n + D], cT[:, :], wmod_sb[:, D * j:D * j + D],
                         start=True, stop=True)
            ins.then_inc(mod_ready, 1)
            pe.wait_ge(mod_stored, 1)
            pe.wait_ge(dve_consts, 11)

            def x1_turn(b, _):
                if before(b) is not None:
                    pe.wait_ge(q2_copied, before(b).after(2, 1))
                pe.wait_ge(xn1_ready, b.after(NT, NT))
                for t in range(NT):
                    ins = tr(ps_t[:, 0, t * P:t * P + P], xn1[:, t, :], ident[:, :])
                ins.then_inc(xT1_ready, 1)

            def qkv(b, _):
                pe.wait_ge(h1_copied, b.after(1, 1))
                if before(b, 2) is not None:
                    pe.wait_ge(comb_steps, before(b, 2).after(7, 4))
                if before(b) is not None:
                    pe.wait_ge(q2_copied, before(b).after(2, 2))
                for t in range(NT):
                    ins = mm(ps_t[:, t, 0:3 * D], h1T[:, t * P:t * P + P], wqkv_sb[:, :],
                             start=True, stop=True)
                ins.then_inc(qkv_ready, 1)

            def transpose_stack(f, block):
                for n in range(2):
                    for t in range(NT):
                        at = n * S + t * P
                        ins = tr(ps_t[:, f % 2, at:at + P],
                                 stack[:, t, (block + n) * P:(block + n + 1) * P].bitcast(F32), ident[:, :])
                return ins

            def stack_turn(b, f):
                if f == 0:
                    pe.wait_ge(lo_done, b.after(2, 2))
                    pe.wait_ge(hi_again, b.after(2, 2))
                    pe.wait_ge(qkv_read, b.after(5, 5))
                if f >= 2:
                    pe.wait_ge(st_copied, b.after(4, f - 1))
                transpose_stack(f, (NA, NA + 2, 0, 2)[f]).then_inc(st_ready, 1)

            def shift(b, _):
                pe.wait_ge(max_lo, b.after(1, 1))
                if before(b) is not None:
                    pe.wait_ge(ldif_done, before(b).after(1, 1))
                    pe.wait_ge(h2_copied, before(b).after(1, 1))
                for f in range(2):
                    transpose_stack(f, 2 * f).then_inc(q2_ready, 1)

            def max_round(b, r):
                g, blocks, t = score_round(r, True)
                if r >= 2:
                    pe.wait_ge(max_taken, b.after(NR, r - 1))
                elif before(b) is not None:
                    pe.wait_ge(exp_done, b.after(NR, r - 1))
                if r == 0:
                    pe.wait_ge(st_copied, b.after(4, 4))
                n, w = score_shape(r, True)
                view = ps_score[r % 2][:, :].rearrange("p (a q) -> p a q", a=n)
                mm(view[:, :, w - P:w], ident_b[:, :], mask_q[:, 0:n * P].rearrange("p (a q) -> p a q", a=n),
                   start=True, stop=False, skip_group_check=True)
                rows = slice(W * g, W * g + KS)
                for m, a in enumerate(blocks):
                    ins = mm(view[:, m, :], qT[b.p][rows, a, t * P:t * P + P], kT[b.p][rows, a, 0:w],
                             start=False, stop=m == n - 1, skip_group_check=True)
                ins.then_inc(max_scores, 1)

            def exp_round(b, r):
                g, blocks, t = score_round(r, False)
                if r == 0:
                    pe.wait_ge(q2_copied, b.after(2, 2))
                if r >= 2:
                    pe.wait_ge(exp_done, b.after(NR, r - 1))
                else:
                    pe.wait_ge(max_taken, b.after(NR, NR - 1 + r))
                n, w = score_shape(r, False)
                rows = slice(W * g, W * g + KM)
                for m, a in enumerate(blocks):
                    ins = mm(ps_score[r % 2][:, m * w:m * w + w], kT[b.p][rows, a, t * P:t * P + P],
                             qT[b.p][rows, a, S - w:S], start=m == 0, stop=m == n - 1, skip_group_check=True)
                ins.then_inc(exp_scores, 1)

            def values(b, r):
                g, blocks, t = score_round(r, False)
                pe.wait_ge(exp_masked, b.after(NR, r + 1))
                if r == 0 and before(b) is not None:
                    pe.wait_ge(o_copied, before(b).after(1, 1))
                n, w = score_shape(r, False)
                for m, a in enumerate(blocks):
                    ins = mm(ps_o[W * a:W * a + W, g // 2, S - w:S], v_ones[b.p][:, t, 4 * a + g, :],
                             probs[r % NP][:, m * w:m * w + w], start=r < 2, stop=r == NR - 1,
                             skip_group_check=True)
                ins.then_inc(pv_done, 1)

            def o_turn(b, _):
                pe.wait_ge(o_copied, b.after(1, 1))
                for t in range(NT):
                    for j in range(2):
                        at = (2 * t + j) * P
                        ins = tr(ps_t[:, 0, at:at + P], oT[:, j, t * P:t * P + P], ident[:, :])
                ins.then_inc(o_turned, 1)

            def on_turn(b, _):
                pe.wait_ge(on_ready, b.after(1, 1))
                for t in range(NT):
                    ins = tr(ps_t[:, 1, t * P:t * P + P],
                             on[:, t * H:t * H + H, :].rearrange("p c d -> p (c d)"), ident[:, :])
                ins.then_inc(on_turned, 1)

            def project(b, _):
                pe.wait_ge(on_copied, b.after(1, 1))
                for t in range(NT):
                    ins = mm(ps_t[:, 0, t * P:t * P + P], onT[:, t * P:t * P + P], wo_sb[:, :],
                             start=True, stop=True)
                ins.then_inc(wo_ready, 1)

            def x2_turn(b, _):
                pe.wait_ge(xn2_ready, b.after(NT, NT))
                for t in range(NT):
                    ins = tr(ps_t[:, 1, t * P:t * P + P], xn2[:, t, :], ident[:, :])
                ins.then_inc(xT2_ready, 1)

            def logits(b, _):
                pe.wait_ge(h2_copied, b.after(1, 1))
                pe.wait_ge(gated_ready, b.after(1, 1))
                for t in range(NT):
                    ins = mm(ps_t[:, 0, t * E:t * E + E], h2T[:, t * P:t * P + P], gw_sb[:, :],
                             start=True, stop=True)
                ins.then_inc(logits_ready, 1)

            def counts(b, _):
                pe.wait_ge(sel_ready, b.after(1, 1))
                if before(b, -1) is not None and not (isinstance(b.i, int) and b.index == B - 1):
                    pe.wait_ge(q2_copied, b.shift(1).after(2, 2))
                if before(b) is not None:
                    pe.wait_ge(comb_steps, before(b).after(7, 7))
                at = ps_t[:, 1, :]
                mm(at[:, 0:E], before_b[:, :], sel_b[:, 0, :], start=True, stop=False)
                mm(at[:, 0:E], ones_b[:, :], sel_past[:, :], start=False, stop=True)
                mm(at[:, E:2 * E], before_b[:, :], sel_b[:, 1, :], start=True, stop=False)
                mm(at[:, E:2 * E], ones_b[:, :], sel_b[:, 0, :], start=False, stop=False)
                mm(at[:, E:2 * E], ones_b[:, :], sel_past[:, :], start=False, stop=True
                   ).then_inc(counts_ready, 1)

            def gate_up(b, k):
                if k == 0:
                    pe.wait_ge(h2_lo_done, b.after(1, 1))
                    if isinstance(b.i, int) and b.index == 0:
                        pe.wait_ge(ffn_split, 2)
                if k >= 2 or before(b) is not None:
                    pe.wait_ge(hid_ready, b.after(NX, k - 1))
                for o in range(2):
                    c0 = (2 * k + o) * I
                    at = ps_gu[k % 2][:, o, :]
                    mm(at, wgu_hi[:, c0:c0 + I], h2_hi[b.p][:, :], start=True, stop=False)
                    mm(at, wgu_hi[:, c0:c0 + I], h2_lo[b.p][:, :], start=False, stop=False)
                    ins = mm(at, wgu_lo[:, c0:c0 + I], h2_hi[b.p][:, :], start=False, stop=True)
                ins.then_inc(gu_ready, 1)

            def down(b, k):
                if k < NSH:
                    pe.wait_ge(hid_ready, b.after(NX, k + 1))
                else:
                    pe.wait_ge(hid_weighed, b.after(E, k - NSH + 1))
                if k == 0 and before(b) is not None:
                    pe.wait_ge(gacc_ready, before(b).after(1, 1))
                for t in range(NT):
                    ins = mm(ps_y[:, 0, t * D:t * D + D], hid[hid_of(b, k)][:, t * P:t * P + P],
                             wd_sb[:, k * D:k * D + D], start=k == 0 and t == 0, stop=k == NX - 1,
                             skip_group_check=True)
                ins.then_inc(down_done, 1)

            run_steps(pe, "pe", {
                ("front", "x1_turn"): x1_turn, ("front", "qkv"): qkv, ("front", "stack"): stack_turn,
                ("mid", "max"): max_round, ("mid", "shift"): shift, ("mid", "exp"): exp_round,
                ("mid", "values"): values, ("tail", "o_turn"): o_turn, ("tail", "on_turn"): on_turn,
                ("tail", "wo"): project, ("tail", "x2_turn"): x2_turn, ("tail", "logits"): logits,
                ("tail", "counts"): counts, ("ffn", "gate_up"): gate_up, ("ffn", "down"): down})


def kernel(L0_attn_x, L0_attn_Wq, L0_attn_Wk, L0_attn_Wv, L0_attn_Wo, L0_ffn_gate_w, L0_ffn_we_gate,
           L0_ffn_we_up, L0_ffn_we_down, L0_ffn_ws_gate, L0_ffn_ws_up, L0_ffn_ws_down, L0_c, L0_wmod):
    import concourse.bacc as bacc
    from concourse.bass_utils import run_bass_kernel_spmd

    arr = lambda a: np.asarray(a)
    inv_freq = (np.float32(1.0) / np.float32(10000.0) ** (np.arange(0, DK, 2, dtype=np.float32) / np.float32(DK)))
    theta = np.arange(S, dtype=np.float32)[:, None] * inv_freq[None, :].astype(np.float32)
    sign = np.tile(np.array([-1.0, 1.0], np.float32), DK // 2)
    rope = np.stack([np.repeat(np.cos(theta), 2, axis=-1), np.repeat(np.sin(theta), 2, axis=-1) * sign],
                    axis=1).astype(np.float32)
    wo = arr(L0_attn_Wo).reshape(NA, 2, 2, DK, D).transpose(1, 0, 2, 3, 4)
    g = np.concatenate([arr(L0_ffn_ws_gate).reshape(NSH, I, D), arr(L0_ffn_we_gate)])
    u = np.concatenate([arr(L0_ffn_ws_up).reshape(NSH, I, D), arr(L0_ffn_we_up)])
    wgu = np.stack([g, u], axis=1).transpose(3, 0, 1, 2).reshape(D, NX * 2 * I)
    d = np.concatenate([arr(L0_ffn_ws_down).reshape(D, NSH, I).transpose(1, 0, 2), arr(L0_ffn_we_down)])
    wd = d.transpose(2, 0, 1).reshape(I, NX * D)
    arrays = {
        "x": arr(L0_attn_x), "wqkv": np.concatenate([arr(L0_attn_Wq), arr(L0_attn_Wk), arr(L0_attn_Wv)], axis=1),
        "wo": wo.reshape(P, D), "gate_w": arr(L0_ffn_gate_w).T, "wgu": wgu, "wd": wd,
        "c": arr(L0_c), "wmod": arr(L0_wmod), "rope": rope,
    }
    nc = bacc.Bacc("TRN2", target_bir_lowering=False, num_devices=1)
    arrays = {f"in_{k}": np.ascontiguousarray(a) for k, a in arrays.items()}
    ins = [nc.dram_tensor(k, a.shape, F32, kind="ExternalInput").ap() for k, a in arrays.items()]
    out = nc.dram_tensor("out_0", (B, S, D), F32, kind="ExternalOutput").ap()
    block_kernel(nc, *ins, out)
    return run_bass_kernel_spmd(nc, [arrays], core_ids=[0]).results[0]["out_0"]
```

```python
from contextlib import ExitStack

import numpy as np

import concourse.bass as bass
from concourse import mybir

F32 = mybir.dt.float32
F32R = mybir.dt.float32r
BF16 = mybir.dt.bfloat16
ALU = mybir.AluOpType
ACT = mybir.ActivationFunctionType
AX_X = mybir.AxisListType.X

P = 128
B, S, D = 16, 256, 128
NT = S // P
H, DK = 16, 8
NA, NG = 4, 4
E, I = 8, 128
NSH = 2
NX = NSH + E
CAP = -(-5 * B * S * 2 // (4 * E))
W = 32
HI0, MID, LAST, MAXC = 0, DK, 2 * DK, 3 * DK
KS = 3 * DK
KM = KS + 2
NR = 12
NP = 8
NV = 8
NH = 4
EPS = 1e-5
NEG = -1e30
SCALE = float(DK) ** -0.5


class Batch:

    def __init__(self, i, c):
        self.i, self.c, self.p = i, c, c % 2

    def shift(self, n):
        return Batch(self.i, self.c + n)

    @property
    def index(self):
        return self.i * 2 + self.c

    def after(self, n, k):
        return self.i * (2 * n) + (n * self.c + k)

    def nth_of_parity(self, n, k):
        return self.i * n + (n * (self.c // 2) + k)


PARTS = {"front": 1, "mid": 0, "tail": -1, "ffn": -2}


FIRST_STEPS = {
    "pe": """
        mid.max.0 mid.max.1 mid.max.2 mid.max.3 mid.max.4 mid.max.5 mid.max.6 tail.o_turn mid.max.7
        mid.max.8 mid.max.9 tail.on_turn mid.max.10 mid.max.11 tail.wo mid.shift.0 mid.shift.1 mid.exp.0
        mid.exp.1 front.x1_turn mid.exp.2 tail.x2_turn front.qkv.0 mid.exp.3 mid.values.0 front.qkv.1
        mid.exp.4 mid.exp.5 mid.values.1 mid.exp.6 tail.logits mid.exp.7 mid.exp.8 mid.values.2 mid.exp.9
        front.stack.0 mid.values.3 mid.exp.10 mid.exp.11 front.stack.1 front.stack.2 mid.values.4
        mid.values.5 mid.values.6 front.stack.3 mid.values.7 tail.counts""",
    "act": """
        tail.o_copy tail.on_copy mid.shift.0 mid.shift.1 mid.exp.0 mid.exp.1 front.h1 mid.exp.2 mid.part
        front.v_copy.0 mid.exp.3 tail.h2 mid.exp.4 mid.exp.5 front.v_copy.1 mid.exp.6 mid.exp.7 front.again
        mid.exp.8 mid.exp.9 front.stack.0 tail.route mid.exp.10 mid.exp.11 front.stack.1 front.stack.2
        front.stack.3 front.part""",
    "dve": """
        mid.max.0 mid.max.1 mid.max.2 mid.max.3 mid.max.4 mid.max.5 mid.max.6 mid.max.7 tail.norm mid.max.8
        mid.max.9 mid.max.10 mid.max.11 tail.residual mid.shift.0 front.stats front.normalise tail.normalise
        front.rope.0 front.rope.1 front.split tail.logits tail.route tail.comb""",
    "pool": """
        front.rstd tail.rstd mid.mask.0 mid.mask.1 mid.mask.2 mid.mask.3 mid.mask.4 mid.mask.5 mid.mask.6
        mid.mask.7 mid.mask.8 mid.mask.9 mid.mask.10 mid.mask.11""",
    "sp": """
        front.load_x mid.load_gates tail.spread""",
}

STEADY_STEPS = {
    "pe": """
        mid.max.0 mid.max.1 ffn.gate_up.0 mid.max.2 mid.max.3 mid.max.4 mid.max.5 ffn.gate_up.1 mid.max.6
        tail.o_turn mid.max.7 mid.max.8 ffn.gate_up.2 mid.max.9 mid.max.10 mid.max.11 tail.on_turn tail.wo
        mid.shift.0 ffn.down.0 ffn.down.1 mid.shift.1 ffn.gate_up.3 mid.exp.0 mid.exp.1 ffn.gate_up.4
        mid.exp.2 mid.exp.3 ffn.down.2 ffn.gate_up.5 mid.exp.4 mid.exp.5 ffn.gate_up.6 front.x1_turn
        ffn.down.3 mid.exp.6 tail.x2_turn front.qkv.0 ffn.gate_up.7 ffn.gate_up.8 tail.logits front.qkv.1
        ffn.down.4 mid.exp.7 ffn.gate_up.9 mid.values.0 ffn.down.5 mid.exp.8 mid.values.1 mid.exp.9
        front.stack.0 ffn.down.6 mid.values.2 mid.exp.10 front.stack.1 ffn.down.7 ffn.down.8 mid.exp.11
        front.stack.2 mid.values.3 ffn.down.9 tail.counts front.stack.3 mid.values.4 mid.values.5
        mid.values.6 mid.values.7""",
    "act": """
        ffn.tanh.0 tail.o_copy tail.on_copy ffn.tanh.1 ffn.tanh.2 mid.shift.0 mid.shift.1 ffn.tanh.3
        mid.exp.0 mid.exp.1 ffn.tanh.4 mid.exp.2 mid.exp.3 ffn.tanh.5 mid.exp.4 front.h1 ffn.tanh.6 tail.h2
        mid.exp.5 ffn.tanh.7 front.v_copy.0 mid.exp.6 mid.part mid.exp.7 front.v_copy.1 front.again
        ffn.tanh.8 mid.exp.8 ffn.tanh.9 front.stack.0 tail.route mid.exp.9 front.stack.1 mid.exp.10
        mid.exp.11 front.stack.2 front.stack.3 front.part""",
    "dve": """
        mid.max.0 mid.max.1 mid.max.2 mid.max.3 mid.max.4 mid.max.5 ffn.hidden.0 mid.max.6 mid.max.7
        tail.norm mid.max.8 mid.max.9 mid.max.10 mid.max.11 mid.shift.0 ffn.hidden.1 tail.residual
        ffn.hidden.2 ffn.hidden.3 front.stats ffn.hidden.4 front.normalise tail.normalise ffn.hidden.5
        ffn.hidden.6 front.rope.0 ffn.hidden.7 front.rope.1 front.split tail.logits ffn.hidden.8
        ffn.hidden.9 tail.route tail.comb ffn.final""",
    "pool": """
        tail.rstd ffn.weigh.2 ffn.weigh.3 front.rstd ffn.weigh.4 ffn.weigh.5 ffn.weigh.6 mid.mask.0
        mid.mask.1 ffn.weigh.7 mid.mask.2 mid.mask.3 mid.mask.4 mid.mask.5 mid.mask.6 mid.mask.7 mid.mask.8
        ffn.weigh.8 mid.mask.9 ffn.weigh.9 mid.mask.10 mid.mask.11""",
    "sp": """
        front.load_x tail.spread mid.load_gates ffn.store""",
}

LAST_STEPS = {
    "pe": """
        mid.max.0 mid.max.1 ffn.gate_up.0 mid.max.2 mid.max.3 mid.max.4 mid.max.5 mid.max.6 mid.max.7
        ffn.gate_up.1 mid.max.8 mid.max.9 tail.o_turn mid.max.10 mid.max.11 ffn.gate_up.2 tail.on_turn
        ffn.down.0 mid.shift.0 tail.wo mid.shift.1 ffn.gate_up.3 ffn.down.1 mid.exp.0 mid.exp.1
        ffn.gate_up.4 mid.exp.2 ffn.gate_up.5 mid.exp.3 mid.exp.4 tail.x2_turn mid.values.0 mid.exp.5
        ffn.gate_up.6 tail.logits mid.exp.6 ffn.down.2 ffn.gate_up.7 ffn.down.3 mid.exp.7 ffn.gate_up.8
        ffn.down.4 mid.values.1 mid.exp.8 tail.counts mid.values.2 mid.exp.9 mid.exp.10 ffn.gate_up.9
        mid.exp.11 ffn.down.5 mid.values.3 ffn.down.6 ffn.down.7 mid.values.4 mid.values.5 mid.values.6
        mid.values.7 ffn.down.8 ffn.down.9""",
    "act": """
        tail.o_copy ffn.tanh.0 ffn.tanh.1 ffn.tanh.2 tail.on_copy mid.shift.0 mid.shift.1 ffn.tanh.3
        mid.exp.0 mid.exp.1 mid.exp.2 ffn.tanh.4 ffn.tanh.5 mid.exp.3 tail.h2 mid.exp.4 ffn.tanh.6 mid.exp.5
        tail.route mid.part ffn.tanh.7 mid.exp.6 mid.exp.7 mid.exp.8 ffn.tanh.8 mid.exp.9 mid.exp.10
        mid.exp.11 ffn.tanh.9""",
    "dve": """
        mid.max.0 mid.max.1 mid.max.2 mid.max.3 mid.max.4 mid.max.5 mid.max.6 mid.max.7 ffn.hidden.0
        mid.max.8 mid.max.9 tail.norm mid.max.10 mid.max.11 mid.shift.0 ffn.hidden.1 ffn.hidden.2
        tail.residual ffn.hidden.3 tail.normalise ffn.hidden.4 ffn.hidden.5 tail.logits ffn.hidden.6
        tail.route ffn.hidden.7 tail.comb ffn.hidden.8 ffn.hidden.9 ffn.final""",
    "pool": """
        tail.rstd mid.mask.0 mid.mask.1 ffn.weigh.2 ffn.weigh.3 mid.mask.2 ffn.weigh.4 ffn.weigh.5
        mid.mask.3 ffn.weigh.6 mid.mask.4 mid.mask.5 mid.mask.6 mid.mask.7 ffn.weigh.7 mid.mask.8 mid.mask.9
        mid.mask.10 mid.mask.11 ffn.weigh.8 ffn.weigh.9""",
    "sp": """
        tail.spread ffn.store mid.load_gates""",
}


def stages_of(order):
    parsed = [word.split(".") for word in order.split()]
    return [(w[0], w[1], int(w[2]) if len(w) > 2 else 0) for w in parsed]


PLANS = [{name: stages_of(order) for name, order in orders.items()}
         for orders in (FIRST_STEPS, STEADY_STEPS, LAST_STEPS)]


def run_steps(eng, name, stages, after=None):
    def step(plan, batch_of):
        for part, stage, k in plan[name]:
            b = batch_of(PARTS[part])
            if b is not None:
                stages[part, stage](b, k)

    def numbered(s):
        step(PLANS[0 if s < 2 else 1 if s < B - 1 else 2],
             lambda n: Batch((s + n) // 2, (s + n) % 2) if 0 <= s + n < B else None)
        if after is not None and s in after:
            after[s]()

    first, end = 4, B - 2
    for s in range(-1, first):
        numbered(s)
    with eng.Fori(0, (end - first) // 2) as i:
        for c in range(first, first + 2):
            step(PLANS[1], lambda n: Batch(i, c + n))
    for s in range(end, B + 2):
        numbered(s)


def before(b, n=1):
    if isinstance(b.i, int) and 2 * b.i + b.c < n:
        return None
    return b.shift(-n)


def score_round(r):
    return (r // 2, range(2 * (r % 2), 2 * (r % 2) + 2)) if r < 8 else (None, range(r - 8, r - 7))


def rounds_of(n):
    return (2 * n, 2 * n + 1) if n < 4 else range(8, NR)


def product_of(r):
    return r // 2 if r < 8 else NV - 1


def score_shape(r):
    return (2, 2 * P) if r < 8 else (4, P)


def block_kernel(nc, x, wqkv, wo, gate_w, wgu, wd, c, wmod, rope, out):
    gate_rows = nc.dram_tensor("gate_rows", [B, 2 * D], F32, kind="Internal").ap()
    comb_rows = nc.dram_tensor("comb_rows", [B, S * E], F32, kind="Internal").ap()
    with ExitStack() as ctx:
        def sb(name, shape, dt=F32):
            return ctx.enter_context(nc.sbuf_tensor(name, shape, dt))

        def sem(name):
            return ctx.enter_context(nc.semaphore(name))

        ps_score = [ctx.enter_context(nc.psum_tensor(f"ps_score{n}", [P, 512], F32)) for n in range(2)]
        ps_gu = [ctx.enter_context(nc.psum_tensor(f"ps_gu{n}", [P, 2, S], F32)) for n in range(2)]
        ps_y = ctx.enter_context(nc.psum_tensor("ps_y", [P, 2, NT * D], F32))
        ps_f = ctx.enter_context(nc.psum_tensor("ps_f", [P, 512], F32))
        ps_t = ctx.enter_context(nc.psum_tensor("ps_t", [P, 512], F32))
        ps_o = ctx.enter_context(nc.psum_tensor("ps_o", [P, 2, S], F32))

        wqkv_sb = sb("wqkv_sb", [P, 3 * D])
        wo_sb = sb("wo_sb", [P, D])
        gw_sb = sb("gw_sb", [P, E])
        wgu_sb = sb("wgu_sb", [P, NX * 2 * I])
        wgu_hi = sb("wgu_hi", [P, NX * 2 * I], F32R)
        wgu_lo = sb("wgu_lo", [P, NX * 2 * I], F32R)
        wd_sb = sb("wd_sb", [P, NX * D])
        wmod_sb = sb("wmod_sb", [P, 6 * D])
        rope_sb = sb("rope_sb", [P, NT, 2, DK])
        ident = sb("ident", [P, P])
        ident_b = sb("ident_b", [P, P], BF16)
        mask_q = sb("mask_q", [P, NA * P], BF16)
        before_b = sb("before_b", [P, P], BF16)
        ones_b = sb("ones_b", [P, P], BF16)
        lower = sb("lower", [P, E, E])
        upper = sb("upper", [P, E, E])
        minus_half = sb("minus_half", [P, NT])
        c_sb = sb("c_sb", [B, D])
        c_th = sb("c_th", [B, D])
        c_silu = sb("c_silu", [B, D])
        cT = sb("cT", [P, B])
        mod = sb("mod", [P, B, 4])
        gate_raw = sb("gate_raw", [B, 2 * D])
        gate_sign = sb("gate_sign", [B, 2 * D])
        gate_mag = sb("gate_mag", [B, 2 * D])
        x_sb = [sb(f"x_sb{n}", [P, NT, D]) for n in range(2)]
        gates = [sb(f"gates{n}", [P, 2 * D]) for n in range(2)]
        st1 = sb("st1", [P, NT, 6])
        mv1 = sb("mv1", [P, NT, 2])
        ve1 = sb("ve1", [P, NT])
        rstd1 = sb("rstd1", [P, NT])
        xn1 = sb("xn1", [P, NT, D])
        h1T = sb("h1T", [P, S])
        qk_cos = sb("qk_cos", [P, NT, 2 * D])
        qk_sin = sb("qk_sin", [P, NT, 2 * D])
        qk = sb("qk", [P, NT, 2 * D])
        stack = sb("stack", [P, NT, 2 * H * W], F32R)
        v_ones = [sb(f"v_ones{n}", [P, NT, H, W]) for n in range(2)]
        qT = [sb(f"qT{n}", [P, NA, S], F32R) for n in range(2)]
        kT = [sb(f"kT{n}", [P, NA, S], F32R) for n in range(2)]
        k_apart = sb("k_apart", [P, NA, NG, P], F32R)
        q_apart = sb("q_apart", [P, NA, NG, P], F32R)
        mx = sb("mx", [P, NT, H])
        probs = [sb(f"probs{n}", [P, 512]) for n in range(NP)]
        oT = sb("oT", [P, 2, S])
        rden = sb("rden", [P, NT * H])
        on = sb("on", [P, NT * H, DK])
        onT = sb("onT", [P, S])
        gated = sb("gated", [P, NT, D])
        x1 = [sb(f"x1_{n}", [P, NT, D]) for n in range(2)]
        st2 = sb("st2", [P, NT, 6])
        mv2 = sb("mv2", [P, NT, 2])
        ve2 = sb("ve2", [P, NT])
        rstd2 = sb("rstd2", [P, NT])
        xn2 = sb("xn2", [P, NT, D])
        h2T = sb("h2T", [P, S])
        h2_hi = [sb(f"h2_hi{n}", [P, S], F32R) for n in range(2)]
        h2_lo = [sb(f"h2_lo{n}", [P, S], F32R) for n in range(2)]
        lmax = sb("lmax", [P, NT])
        ldif = sb("ldif", [P, NT, E])
        ex = sb("ex", [P, NT, E])
        ge = sb("ge", [P, NT, E, E])
        gt = sb("gt", [P, NT, E, E])
        ge_l = sb("ge_l", [P, NT, E, E])
        gt_u = sb("gt_u", [P, NT, E, E])
        beats = sb("beats", [P, NT, E, E])
        rank = sb("rank", [P, NT, E])
        sel = sb("sel", [P, NT, E])
        sel_b = sb("sel_b", [P, NT, E], BF16)
        sel_past = sb("sel_past", [P, E], BF16)
        esum = sb("esum", [P, NT])
        esel = sb("esel", [P, NT, E])
        wsum = sb("wsum", [P, NT])
        wden = sb("wden", [P, NT])
        wrec = sb("wrec", [P, NT])
        ekeep = sb("ekeep", [P, NT, E])
        comb = [sb(f"comb{n}", [P, NT, E]) for n in range(2)]
        th = [sb(f"th{n}", [P, S]) for n in range(2)]
        silu = [sb(f"silu{n}", [P, S]) for n in range(2)]
        hid = [sb(f"hid{n}", [P, S]) for n in range(NH)]
        comb_all = [sb(f"comb_all{n}", [P, S * E]) for n in range(2)]
        gacc = sb("gacc", [P, NT, D])
        out_sb = [sb(f"out_sb{n}", [P, NT, D]) for n in range(2)]

        passed = sem("passed")
        c_loaded, wmod_loaded, weights_loaded, ffn_loaded = (
            sem("c_loaded"), sem("wmod_loaded"), sem("weights_loaded"), sem("ffn_loaded"))
        c_tanh, c_done, cT_ready, cT_copied, mod_ready, mod_stored = (
            sem("c_tanh"), sem("c_done"), sem("cT_ready"), sem("cT_copied"), sem("mod_ready"), sem("mod_stored"))
        setup_pool, setup_dve, gates_computed, gates_written = (
            sem("setup_pool"), sem("setup_dve"), sem("gates_computed"), sem("gates_written"))
        ident_ready, apart_clear, pool_consts, consts_ready, ffn_split = (
            sem("ident_ready"), sem("apart_clear"), sem("pool_consts"), sem("consts_ready"), sem("ffn_split"))
        x_loaded = [sem(f"x_loaded{n}") for n in range(2)]
        gates_loaded = [sem(f"gates_loaded{n}") for n in range(2)]
        ln1_stats, ln1_mv, ln1_var, ln1_rstd, xn1_ready = (
            sem("ln1_stats"), sem("ln1_mv"), sem("ln1_var"), sem("ln1_rstd"), sem("xn1_ready"))
        xT1_ready, h1_copied, qkv_ready = sem("xT1_ready"), sem("h1_copied"), sem("qkv_ready")
        qk_read, v_copied, rope_done, hi_done, lo_done, hi_again = (
            sem("qk_read"), sem("v_copied"), sem("rope_done"), sem("hi_done"), sem("lo_done"), sem("hi_again"))
        st_ready, st_copied = sem("st_ready"), sem("st_copied")
        max_scores, max_taken = sem("max_scores"), sem("max_taken")
        k_parted, q_parted = sem("k_parted"), sem("q_parted")
        max_hi, max_lo, q2_ready, q2_copied = sem("max_hi"), sem("max_lo"), sem("q2_ready"), sem("q2_copied")
        exp_scores, exp_done, pv_done = sem("exp_scores"), sem("exp_done"), sem("pv_done")
        exp_masked = sem("exp_masked")
        o_copied, o_turned, den_rec, on_ready, on_turned, on_copied = (
            sem("o_copied"), sem("o_turned"), sem("den_rec"), sem("on_ready"), sem("on_turned"), sem("on_copied"))
        wo_ready, gated_ready, x1_ready = sem("wo_ready"), sem("gated_ready"), sem("x1_ready")
        ln2_stats, ln2_mv, ln2_var, ln2_rstd, xn2_ready = (
            sem("ln2_stats"), sem("ln2_mv"), sem("ln2_var"), sem("ln2_rstd"), sem("xn2_ready"))
        xT2_ready, h2_copied, h2_hi_done, h2_lo_done = (
            sem("xT2_ready"), sem("h2_copied"), sem("h2_hi_done"), sem("h2_lo_done"))
        logits_ready, lmax_done, ldif_done, route_exp = (
            sem("logits_ready"), sem("lmax_done"), sem("ldif_done"), sem("route_exp"))
        rank_steps, sel_ready, counts_ready, comb_steps = (
            sem("rank_steps"), sem("sel_ready"), sem("counts_ready"), sem("comb_steps"))
        gu_ready, th_done, silu_done, hid_ready = (
            sem("gu_ready"), sem("th_done"), sem("silu_done"), sem("hid_ready"))
        hid_weighed, down_done = sem("hid_weighed"), sem("down_done")
        comb_stored, comb_spread = ([sem(f"{n}{p}") for p in range(2)] for n in ("comb_stored", "comb_spread"))
        gacc_ready, out_ready = sem("gacc_ready"), sem("out_ready")
        out_stored = [sem(f"out_stored{n}") for n in range(2)]

        heads = lambda t: t.rearrange("p t (h w) -> p t h w", w=W)

        def hid_of(b, k):
            return (NX % NH * b.p + k) % NH


        block = ctx.enter_context(nc.Block())

        def wait_apart(eng, signal, value):
            eng.wait_ge(signal, value)
            eng.sem_inc(passed, 1)

        @block.sync
        def _(sp):
            sp.dma_start(c_sb[:, :], c).then_inc(c_loaded, 16)
            sp.dma_start(x_sb[0][:, :, :], x[0].rearrange("(t p) d -> p t d", p=P)).then_inc(x_loaded[0], 16)
            sp.dma_start(wmod_sb[:, :], wmod).then_inc(wmod_loaded, 16)
            for dst, src in ((wqkv_sb[:, :], wqkv),
                             (rope_sb[:, :, :, :], rope.rearrange("(t p) a d -> p t a d", p=P)),
                             (wo_sb[:, :], wo), (gw_sb[:, :], gate_w)):
                sp.dma_start(dst, src).then_inc(weights_loaded, 16)

            def feed_forward_weights():
                sp.dma_start(wgu_sb[:, :], wgu).then_inc(ffn_loaded, 16)
                sp.dma_start(wd_sb[:, :], wd).then_inc(ffn_loaded, 16)
                sp.wait_ge(gates_computed, 1)
                sp.dma_start(gate_rows, gate_mag[:, :]).then_inc(gates_written, 16)
                sp.wait_ge(gates_written, 16)

            def load_x(b, _):
                if isinstance(b.i, int) and b.index == 0:
                    return
                old = before(b, 2)
                if old is not None:
                    sp.wait_ge(x1_ready, old.after(1, 1))
                sp.dma_start(x_sb[b.p][:, :, :],
                             x[bass.ds(b.index, 1)].rearrange("o (t p) d -> p (o t) d", p=P)
                             ).then_inc(x_loaded[b.p], 16)

            def load_gates(b, _):
                old = before(b, 2)
                if old is not None:
                    sp.wait_ge(out_ready, old.after(1, 1))
                sp.dma_start(gates[b.p][:, :], gate_rows[bass.ds(b.index, 1)].to_broadcast([P, 2 * D])
                             ).then_inc(gates_loaded[b.p], 16)

            def spread(b, _):
                wait_apart(sp, comb_steps, b.after(7, 7))
                sp.dma_start(comb_rows[bass.ds(b.index, 1)].rearrange("o (p c) -> p (o c)", p=P),
                             comb[b.p][:, :, :].rearrange("p t e -> p (t e)")).then_inc(comb_stored[b.p], 16)
                wait_apart(sp, comb_stored[b.p], b.nth_of_parity(16, 16))
                old = before(b, 2)
                if old is not None:
                    wait_apart(sp, hid_weighed, old.after(E, E))
                sp.dma_start(comb_all[b.p][:, :], comb_rows[bass.ds(b.index, 1)].to_broadcast([P, S * E])
                             ).then_inc(comb_spread[b.p], 16)

            def store(b, _):
                sp.wait_ge(out_ready, b.after(1, 1))
                sp.dma_start(out[bass.ds(b.index, 1)].rearrange("o (t p) d -> p (o t) d", p=P),
                             out_sb[b.p][:, :, :]).then_inc(out_stored[b.p], 16)

            run_steps(sp, "sp", {("front", "load_x"): load_x, ("mid", "load_gates"): load_gates,
                                 ("tail", "spread"): spread, ("ffn", "store"): store}, {-1: feed_forward_weights})
            for n in range(2):
                sp.wait_ge(out_stored[n], 16 * (B // 2))

        @block.gpsimd
        def _(pool):
            n = 0

            def link(ins):
                nonlocal n
                n += 1
                ins.then_inc(setup_pool, 1)
                pool.wait_ge(setup_pool, n)

            g = nc.gpsimd

            def ones_of(vo):
                pair = vo[:, :, :, :].rearrange("p t (c o) w -> p t c o w", o=2)
                for o in range(2):
                    for t in range(NT):
                        g.memset(pair[:, t, :, o, 16 * o + DK:16 * o + 2 * DK], 1.0).then_inc(pool_consts, 1)

            def rstd1_of(b, _):
                wait_apart(pool, ln1_mv, b.after(1, 1))
                g.tensor_scalar(ve1[:, :], mv1[:, :, 1], EPS, None, ALU.add).then_inc(ln1_var, 1)
                pool.wait_ge(ln1_var, b.after(1, 1))
                g.tensor_tensor(rstd1[:, :], ve1[:, :], minus_half[:, :], ALU.pow).then_inc(ln1_rstd, 1)

            link(g.memset(ident[:, :], 0.0))
            link(g.affine_select(out=ident[:, :], in_=ident[:, :], compare_op=ALU.not_equal, fill=1.0,
                                 base=0, pattern=[[-1, P]], channel_multiplier=1))
            g.tensor_copy(ident_b[:, :], ident[:, :]).then_inc(ident_ready, 1)
            g.memset(minus_half[:, :], -0.5).then_inc(pool_consts, 1)
            link(g.memset(stack[:, :, :].bitcast(F32), 0.0))
            g.memset(heads(stack[:, :, :])[:, :, H:2 * H, MAXC:MAXC + 2].bitcast(F32), 1.0).then_inc(pool_consts, 1)
            rstd1_of(Batch(0, 0), 0)
            link(g.memset(v_ones[0][:, :, :, :], 0.0))
            ones_of(v_ones[0])
            link(g.memset(mask_q[:, :], 0.0))
            g.affine_select(out=mask_q[:, :], in_=mask_q[:, :], compare_op=ALU.is_ge, fill=NEG, base=0,
                            pattern=[[0, NA], [-1, P]], channel_multiplier=1).then_inc(consts_ready, 1)
            g.memset(k_apart[:, :, :, :].bitcast(F32), 0.0).then_inc(apart_clear, 1)
            g.memset(q_apart[:, :, :, :].bitcast(F32), 0.0).then_inc(apart_clear, 1)
            link(g.memset(v_ones[1][:, :, :, :], 0.0))
            ones_of(v_ones[1])

            def routing_constants():
                link(g.memset(before_b[:, :], 1.0))
                g.affine_select(out=before_b[:, :], in_=before_b[:, :], compare_op=ALU.is_gt, fill=0.0, base=0,
                                pattern=[[1, P]], channel_multiplier=-1).then_inc(consts_ready, 1)
                g.memset(ones_b[:, :], 1.0).then_inc(consts_ready, 1)
                g.memset(sel_past[:, :], 0.0).then_inc(consts_ready, 1)
                link(g.memset(lower[:, :, :], 1.0))
                g.affine_select(out=lower[:, :, :], in_=lower[:, :, :], compare_op=ALU.is_gt, fill=0.0, base=0,
                                pattern=[[1, E], [-1, E]], channel_multiplier=0).then_inc(consts_ready, 1)
                link(g.memset(upper[:, :, :], 1.0))
                g.affine_select(out=upper[:, :, :], in_=upper[:, :, :], compare_op=ALU.is_gt, fill=0.0, base=0,
                                pattern=[[-1, E], [1, E]], channel_multiplier=0).then_inc(consts_ready, 1)

            def rstd2_of(b, _):
                wait_apart(pool, ln2_mv, b.after(1, 1))
                g.tensor_scalar(ve2[:, :], mv2[:, :, 1], EPS, None, ALU.add).then_inc(ln2_var, 1)
                pool.wait_ge(ln2_var, b.after(1, 1))
                g.tensor_tensor(rstd2[:, :], ve2[:, :], minus_half[:, :], ALU.pow).then_inc(ln2_rstd, 1)

            def mask(b, r):
                n, w = score_shape(r)
                wait_apart(pool, exp_done, b.after(NR, r + 1))
                v = probs[r % NP][:, :].rearrange("p (a q) -> p a q", a=n)[:, :, 0:P]
                g.affine_select(out=v, in_=v, compare_op=ALU.is_ge, fill=0.0, base=0,
                                pattern=[[0, n], [1, P]], channel_multiplier=-1).then_inc(exp_masked, 1)

            def weigh(b, k):
                if k == NSH:
                    pool.wait_ge(comb_spread[b.p], b.nth_of_parity(16, 16))
                pool.wait_ge(hid_ready, b.after(NX, k + 1))
                h = hid[hid_of(b, k)][:, :].rearrange("i (t p) -> i t p", t=NT)
                w = comb_all[b.p][:, :].rearrange("i (p t e) -> i e t p", t=NT, e=E)[:, k - NSH]
                g.tensor_tensor(h, h, w, ALU.mult).then_inc(hid_weighed, 1)

            def front_rstd(b, _):
                if not (isinstance(b.i, int) and b.index == 0):
                    rstd1_of(b, 0)

            run_steps(pool, "pool", {("ffn", "weigh"): weigh,
                                     ("front", "rstd"): front_rstd, ("tail", "rstd"): rstd2_of,
                                     ("mid", "mask"): mask}, {-1: routing_constants})

        @block.scalar
        def _(act):
            s = nc.scalar
            act.wait_ge(c_loaded, 16)
            s.activation(c_th[:, :], c_sb[:, :], ACT.Tanh, scale=0.5).then_inc(c_tanh, 1)

            def transposed(dst, src, b, which):
                m = mod[:, bass.ds(b.index, 1), :]
                return s.activation(dst, src, ACT.Identity,
                                    scale=m[:, :, which:which + 1].rearrange("p o k -> p (o k)"),
                                    bias=m[:, :, which + 1:which + 2].rearrange("p o k -> p (o k)"))

            def h1(b, _):
                if isinstance(b.i, int) and b.index == 0:
                    act.wait_ge(mod_stored, 1)
                act.wait_ge(xT1_ready, b.after(1, 1))
                transposed(h1T[:, :], ps_f[:, 0:S], b, 0).then_inc(h1_copied, 1)

            def v_copy(b, t):
                act.wait_ge(qk_read, b.after(3 * NT, 3 * t + 3))
                if t == 0:
                    if isinstance(b.i, int) and b.index == 0:
                        act.wait_ge(pool_consts, 10)
                    if before(b, 2) is not None:
                        act.wait_ge(pv_done, before(b, 2).after(NV, NV))
                val = ps_f[:, 2 * D:3 * D].rearrange("p (c o d) -> p c o d", o=2, d=DK)
                vo = v_ones[b.p][:, t, :, :].rearrange("p (c o) w -> p c o w", o=2)
                for o in range(2):
                    s.activation(vo[:, :, o, 16 * o:16 * o + DK], val[:, :, o, :], ACT.Copy).then_inc(v_copied, 1)

            def again(b, _):
                act.wait_ge(hi_done, b.after(1, 1))
                st = heads(stack[:, :, :])
                for o, slot in ((0, MID), (H, LAST)):
                    s.activation(st[:, :, o:o + H, slot:slot + DK], st[:, :, o:o + H, HI0:HI0 + DK].bitcast(F32),
                                 ACT.Copy).then_inc(hi_again, 1)

            def stack_copy(b, f):
                act.wait_ge(st_ready, b.after(4, f + 1))
                dst = (kT, kT, qT, qT)[f][b.p][:, 2 * (f % 2):2 * (f % 2) + 2, :]
                s.activation(dst, ps_f[:, :].rearrange("p (a q) -> p a q", a=2),
                             ACT.Copy).then_inc(st_copied, 1)

            def part(dst, src, rows, done):
                for g in range(NG):
                    at = slice(W * g, W * g + rows)
                    s.activation(dst[at, :, g, :], src[at, :, :], ACT.Copy).then_inc(done, 1)

            def part_keys(b, _):
                act.wait_ge(st_copied, b.after(4, 2))
                if before(b) is None:
                    act.wait_ge(apart_clear, 2)
                else:
                    act.wait_ge(max_scores, before(b).after(NR, NR))
                part(k_apart, kT[b.p][:, :, 0:P], KS, k_parted)

            def part_queries(b, _):
                act.wait_ge(q2_copied, b.after(2, 2))
                if before(b) is not None:
                    act.wait_ge(exp_scores, before(b).after(NR, NR))
                part(q_apart, qT[b.p][:, :, P:2 * P], KM, q_parted)

            def shift(b, f):
                act.wait_ge(q2_ready, b.after(2, f + 1))
                s.activation(qT[b.p][:, 2 * f:2 * f + 2, :], ps_f[:, :].rearrange("p (a q) -> p a q", a=2),
                             ACT.Copy).then_inc(q2_copied, 1)

            def exp(b, r):
                act.wait_ge(exp_scores, b.after(NR, r + 1))
                if r >= NP:
                    act.wait_ge(pv_done, b.after(NV, product_of(r - NP) + 1))
                elif before(b) is not None:
                    last = r + NP if r + NP < NR else r
                    act.wait_ge(pv_done, before(b).after(NV, product_of(last) + 1))
                s.activation(probs[r % NP][:, :], ps_score[r % 2][:, :], ACT.Exp,
                             scale=SCALE).then_inc(exp_done, 1)

            def o_copy(b, _):
                act.wait_ge(pv_done, b.after(NV, NV))
                s.activation(oT[:, :, :], ps_o[:, :, :], ACT.Copy).then_inc(o_copied, 1)

            def on_copy(b, _):
                act.wait_ge(on_turned, b.after(1, 1))
                s.activation(onT[:, :], ps_t[:, 0:S], ACT.Copy).then_inc(on_copied, 1)

            def h2(b, _):
                act.wait_ge(xT2_ready, b.after(1, 1))
                transposed(h2_hi[b.p][:, :], ps_t[:, 0:S], b, 2).then_inc(h2_hi_done, 1)
                transposed(h2T[:, :], ps_t[:, 0:S], b, 2).then_inc(h2_copied, 1)

            def route(b, _):
                act.wait_ge(ldif_done, b.after(1, 1))
                s.activation(ex[:, :, :], ldif[:, :, :], ACT.Exp).then_inc(route_exp, 1)

            def tanh(b, k):
                act.wait_ge(gu_ready, b.after(NX, k + 1))
                s.activation(th[k % 2][:, :], ps_gu[k % 2][:, 0, :], ACT.Tanh, scale=0.5).then_inc(th_done, 1)

            run_steps(act, "act", {
                ("front", "h1"): h1, ("front", "v_copy"): v_copy, ("front", "again"): again,
                ("front", "stack"): stack_copy, ("front", "part"): part_keys,
                ("mid", "shift"): shift, ("mid", "part"): part_queries,
                ("mid", "exp"): exp, ("tail", "o_copy"): o_copy, ("tail", "on_copy"): on_copy,
                ("tail", "h2"): h2, ("tail", "route"): route, ("ffn", "tanh"): tanh})

        @block.vector
        def _(dve):
            v = nc.vector
            n = 0

            def link(ins):
                nonlocal n
                n += 1
                ins.then_inc(setup_dve, 1)
                dve.wait_ge(setup_dve, n)

            def layer_stats(b, src, st, mv, stats, done):
                for t in range(NT):
                    v.bn_stats(st[:, t, :], src[:, t, :]).then_inc(stats, 1)
                wait_apart(dve, stats, b.after(NT, NT))
                for t in range(NT):
                    ins = v.bn_aggr(mv[:, t, :], st[:, t, :])
                ins.then_inc(done, 1)

            def first_stats():
                layer_stats(Batch(0, 0), x_sb[0], st1, mv1, ln1_stats, ln1_mv)

            dve.wait_ge(c_tanh, 1)
            link(v.tensor_scalar(c_th[:, :], c_th[:, :], 1.0, 0.5, ALU.add, ALU.mult))
            v.tensor_tensor(c_silu[:, :], c_th[:, :], c_sb[:, :], ALU.mult).then_inc(c_done, 1)
            dve.wait_ge(cT_ready, 1)
            v.tensor_copy(cT[:, :], ps_o[:, 0, 0:B]).then_inc(cT_copied, 1)
            dve.wait_ge(x_loaded[0], 16)
            first_stats()
            dve.wait_ge(mod_ready, 1)
            mv = ps_o[:, 1, 0:4 * B].rearrange("p (k b) -> p b k", b=B)
            for k in range(4):
                ins = v.tensor_scalar(mod[:, :, k], mv[:, :, k], 1.0 if k % 2 == 0 else 0.0, None, ALU.add)
                if k < 3:
                    link(ins)
            ins.then_inc(mod_stored, 1)

            def gate_rows_of():
                dve.wait_ge(mod_ready, 2)
                v.tensor_copy(gate_raw[:, :], ps_o[0:B, 0, 0:2 * D]).then_inc(mod_stored, 1)
                dve.wait_ge(mod_stored, 2)
                link(v.tensor_scalar(gate_sign[:, :], gate_raw[:, :], 0.0, 2.0, ALU.is_ge, ALU.mult))
                link(v.tensor_scalar(gate_mag[:, :], gate_raw[:, :], -1.0, None, ALU.mult))
                link(v.tensor_tensor(gate_raw[:, :], gate_mag[:, :], gate_raw[:, :], ALU.max))
                link(v.tensor_scalar(gate_raw[:, :], gate_raw[:, :], 0.25, None, ALU.max))
                v.scalar_tensor_tensor(gate_mag[:, :], gate_sign[:, :], -1.0, gate_raw[:, :],
                                       ALU.add, ALU.mult).then_inc(gates_computed, 1)
                dve.wait_ge(consts_ready, 6)

            def split_weights():
                dve.wait_ge(ffn_loaded, 32)
                v.tensor_copy(wgu_hi[:, :], wgu_sb[:, :]).then_inc(ffn_split, 1)
                dve.wait_ge(ffn_split, 1)
                v.tensor_tensor(wgu_lo[:, :], wgu_sb[:, :], wgu_hi[:, :].bitcast(F32),
                                ALU.subtract).then_inc(ffn_split, 1)

            def normalise(b, src, mv, rstd, dst, ready, done):
                dve.wait_ge(ready, b.after(1, 1))
                for t in range(NT):
                    v.tensor_scalar(dst[:, t, :], src[:, t, :], mv[:, t, 0:1], rstd[:, t:t + 1],
                                    ALU.subtract, ALU.mult).then_inc(done, 1)

            def front_stats(b, _):
                if isinstance(b.i, int) and b.index == 0:
                    return
                dve.wait_ge(x_loaded[b.p], b.nth_of_parity(16, 16))
                layer_stats(b, x_sb[b.p], st1, mv1, ln1_stats, ln1_mv)

            def front_normalise(b, _):
                normalise(b, x_sb[b.p], mv1, rstd1, xn1, ln1_rstd, xn1_ready)

            def rope_turn(b, t):
                raw = ps_f[:, 0:2 * D].rearrange("p (h d) -> p h d", d=DK)
                cos = rope_sb[:, t, 0, :].unsqueeze(1).to_broadcast([P, 2 * H, DK])
                sin = rope_sb[:, t, 1, :].unsqueeze(1).to_broadcast([P, 2 * H, DK])
                dve.wait_ge(qkv_ready, b.after(NT, t + 1))
                v.tensor_tensor(qk_cos[:, t, :].rearrange("p (h d) -> p h d", d=DK), raw, cos,
                                ALU.mult).then_inc(qk_read, 1)
                sn = qk_sin[:, t, :].rearrange("p (h d) -> p h d", d=DK)
                for o in range(2):
                    v.tensor_tensor(sn[:, :, o::2], raw[:, :, 1 - o::2], sin[:, :, o::2],
                                    ALU.mult).then_inc(qk_read, 1)
                if t < NT - 1:
                    return
                dve.wait_ge(qk_read, b.after(3 * NT, 3 * NT))
                v.tensor_tensor(qk[:, :, :], qk_cos[:, :, :], qk_sin[:, :, :], ALU.add).then_inc(rope_done, 1)

            def split(b, _):
                st = heads(stack[:, :, :])
                dve.wait_ge(rope_done, b.after(1, 1))
                if isinstance(b.i, int) and b.index == 0:
                    dve.wait_ge(pool_consts, 10)
                if before(b) is not None:
                    dve.wait_ge(q2_ready, before(b).after(2, 2))
                qk4 = qk[:, :, :].rearrange("p t (h d) -> p t h d", d=DK)
                v.tensor_copy(st[:, :, :, HI0:HI0 + DK], qk4).then_inc(hi_done, 1)
                dve.wait_ge(hi_done, b.after(1, 1))
                for o, slot in ((0, LAST), (H, MID)):
                    v.tensor_tensor(st[:, :, o:o + H, slot:slot + DK], qk4[:, :, o:o + H, :],
                                    st[:, :, o:o + H, HI0:HI0 + DK].bitcast(F32),
                                    ALU.subtract).then_inc(lo_done, 1)

            def row_max(b, r):
                dve.wait_ge(max_scores, b.after(NR, r + 1))
                g, blocks = score_round(r)
                n, w = score_shape(r)
                dst = (mx[:, 0, NG * blocks[0]:NG * blocks[0] + NG] if g is None else
                       mx[:, 1, :].rearrange("p (a g) -> p a g", g=NG)[:, blocks[0]:blocks[-1] + 1, g])
                v.reduce_max(dst, ps_score[r % 2][:, :].rearrange("p (a q) -> p a q", a=n),
                             AX_X).then_inc(max_taken, 1)

            def shift(b, _):
                q = heads(stack[:, :, :])[:, :, 0:H, :]
                dve.wait_ge(max_taken, b.after(NR, NR))
                v.tensor_scalar(q[:, :, :, MAXC], mx[:, :, :], -1.0, None, ALU.mult).then_inc(max_hi, 1)
                dve.wait_ge(max_hi, b.after(1, 1))
                v.scalar_tensor_tensor(q[:, :, :, MAXC + 1], mx[:, :, :], -1.0,
                                       q[:, :, :, MAXC].bitcast(F32), ALU.mult,
                                       ALU.subtract).then_inc(max_lo, 1)

            def norm(b, _):
                dve.wait_ge(o_turned, b.after(1, 1))
                o = ps_t[:, :].rearrange("p (c w) -> p c w", w=2 * DK)
                v.reciprocal(rden[:, :], o[:, :, DK]).then_inc(den_rec, 1)
                dve.wait_ge(den_rec, b.after(1, 1))
                v.tensor_tensor(on[:, :, :], o[:, :, 0:DK], rden[:, :].unsqueeze(2).to_broadcast([P, NT * H, DK]),
                                ALU.mult).then_inc(on_ready, 1)

            def residual(b, _):
                dve.wait_ge(gates_loaded[b.p], b.nth_of_parity(16, 16))
                dve.wait_ge(wo_ready, b.after(1, 1))
                ga = gates[b.p][:, 0:D].unsqueeze(1).to_broadcast([P, NT, D])
                v.tensor_tensor(gated[:, :, :], ps_t[:, 0:S].rearrange("p (t d) -> p t d", t=NT),
                                ga, ALU.mult).then_inc(gated_ready, 1)
                dve.wait_ge(gated_ready, b.after(1, 1))
                v.tensor_tensor(x1[b.p][:, :, :], gated[:, :, :], x_sb[b.p][:, :, :], ALU.add
                                ).then_inc(x1_ready, 1)
                dve.wait_ge(x1_ready, b.after(1, 1))
                layer_stats(b, x1[b.p], st2, mv2, ln2_stats, ln2_mv)

            def tail_normalise(b, _):
                normalise(b, x1[b.p], mv2, rstd2, xn2, ln2_rstd, xn2_ready)

            def logits(b, _):
                dve.wait_ge(h2_hi_done, b.after(1, 1))
                dve.wait_ge(h2_copied, b.after(1, 1))
                v.tensor_tensor(h2_lo[b.p][:, :], h2T[:, :], h2_hi[b.p][:, :].bitcast(F32),
                                ALU.subtract).then_inc(h2_lo_done, 1)
                dve.wait_ge(logits_ready, b.after(1, 1))
                lg = ps_t[:, 0:NT * E].rearrange("p (t e) -> p t e", t=NT)
                v.reduce_max(lmax[:, :], lg, AX_X).then_inc(lmax_done, 1)
                dve.wait_ge(lmax_done, b.after(1, 1))
                v.tensor_tensor(ldif[:, :, :], lg, lmax[:, :].unsqueeze(2).to_broadcast([P, NT, E]),
                                ALU.subtract).then_inc(ldif_done, 1)

            def route(b, _):
                dve.wait_ge(route_exp, b.after(1, 1))
                other = ex[:, :, :].unsqueeze(2).to_broadcast([P, NT, E, E])
                own = ex[:, :, :].unsqueeze(3).to_broadcast([P, NT, E, E])
                for t in range(NT):
                    v.tensor_tensor(ge[:, t], other[:, t], own[:, t], ALU.is_ge).then_inc(rank_steps, 1)
                    v.tensor_tensor(gt[:, t], other[:, t], own[:, t], ALU.is_gt).then_inc(rank_steps, 1)
                v.reduce_sum(esum[:, :], ex[:, :, :], AX_X).then_inc(rank_steps, 1)
                dve.wait_ge(rank_steps, b.after(11, 4))
                low = lower[:, :, :].unsqueeze(1).to_broadcast([P, NT, E, E])
                upp = upper[:, :, :].unsqueeze(1).to_broadcast([P, NT, E, E])
                v.tensor_tensor(ge_l[:, :, :, :], ge[:, :, :, :], low, ALU.mult).then_inc(rank_steps, 1)
                v.tensor_tensor(gt_u[:, :, :, :], gt[:, :, :, :], upp, ALU.mult).then_inc(rank_steps, 1)
                dve.wait_ge(rank_steps, b.after(11, 7))
                v.tensor_tensor(beats[:, :, :, :], ge_l[:, :, :, :], gt_u[:, :, :, :], ALU.add
                                ).then_inc(rank_steps, 1)
                dve.wait_ge(rank_steps, b.after(11, 8))
                v.reduce_sum(rank[:, :, :], beats[:, :, :, :], AX_X).then_inc(rank_steps, 1)
                dve.wait_ge(rank_steps, b.after(11, 9))
                v.tensor_scalar(sel[:, :, :], rank[:, :, :], 2.0, None, ALU.is_lt).then_inc(rank_steps, 1)
                v.tensor_scalar(sel_b[:, :, :], rank[:, :, :], 2.0, None, ALU.is_lt).then_inc(sel_ready, 1)
                dve.wait_ge(rank_steps, b.after(11, 10))
                v.tensor_tensor(esel[:, :, :], ex[:, :, :], sel[:, :, :], ALU.mult).then_inc(rank_steps, 1)

            def combine_weights(b, _):
                dve.wait_ge(rank_steps, b.after(11, 11))
                v.reduce_sum(wsum[:, :], esel[:, :, :], AX_X).then_inc(comb_steps, 1)
                dve.wait_ge(comb_steps, b.after(7, 1))
                v.scalar_tensor_tensor(wden[:, :], esum[:, :], 1e-20, wsum[:, :], ALU.mult, ALU.add
                                       ).then_inc(comb_steps, 1)
                dve.wait_ge(comb_steps, b.after(7, 2))
                v.reciprocal(wrec[:, :], wden[:, :]).then_inc(comb_steps, 1)
                dve.wait_ge(counts_ready, b.after(1, 1))
                pos = ps_t[:, 0:NT * E].rearrange("p (t e) -> p t e", t=NT)
                v.scalar_tensor_tensor(ekeep[:, :, :], pos, float(CAP), esel[:, :, :], ALU.is_lt, ALU.mult
                                       ).then_inc(comb_steps, 1)
                v.tensor_tensor(sel_past[:, :], sel_past[:, :], sel_b[:, 0, :], ALU.add).then_inc(comb_steps, 1)
                dve.wait_ge(comb_steps, b.after(7, 5))
                v.tensor_tensor(sel_past[:, :], sel_past[:, :], sel_b[:, 1, :], ALU.add).then_inc(comb_steps, 1)
                v.tensor_tensor(comb[b.p][:, :, :], ekeep[:, :, :],
                                wrec[:, :].unsqueeze(2).to_broadcast([P, NT, E]), ALU.mult).then_inc(comb_steps, 1)

            def hidden(b, k):
                dve.wait_ge(th_done, b.after(NX, k + 1))
                v.scalar_tensor_tensor(silu[k % 2][:, :], th[k % 2][:, :], 1.0, ps_gu[k % 2][:, 0, :],
                                       ALU.add, ALU.mult).then_inc(silu_done, 1)
                dve.wait_ge(silu_done, b.after(NX, k + 1))
                if k >= NH or before(b) is not None:
                    dve.wait_ge(down_done, b.after(NX, k - NH + 1))
                v.scalar_tensor_tensor(hid[hid_of(b, k)][:, :], silu[k % 2][:, :], 0.5, ps_gu[k % 2][:, 1, :],
                                       ALU.mult, ALU.mult).then_inc(hid_ready, 1)

            def final(b, _):
                dve.wait_ge(down_done, b.after(NX, NX))
                gb = gates[b.p][:, D:2 * D].unsqueeze(1).to_broadcast([P, NT, D])
                y = ps_y[:, 0, :].rearrange("p (t d) -> p t d", t=NT)
                v.tensor_tensor(gacc[:, :, :], y, gb, ALU.mult).then_inc(gacc_ready, 1)
                dve.wait_ge(gacc_ready, b.after(1, 1))
                old = before(b, 2)
                if old is not None:
                    dve.wait_ge(out_stored[b.p], old.nth_of_parity(16, 16))
                v.tensor_tensor(out_sb[b.p][:, :, :], gacc[:, :, :], x1[b.p][:, :, :],
                                ALU.add).then_inc(out_ready, 1)

            run_steps(dve, "dve", {
                ("front", "stats"): front_stats, ("front", "normalise"): front_normalise,
                ("front", "rope"): rope_turn, ("front", "split"): split,
                ("mid", "max"): row_max, ("mid", "shift"): shift,
                ("tail", "norm"): norm, ("tail", "residual"): residual, ("tail", "normalise"): tail_normalise,
                ("tail", "logits"): logits, ("tail", "route"): route, ("tail", "comb"): combine_weights,
                ("ffn", "hidden"): hidden, ("ffn", "final"): final},
                {-1: gate_rows_of, 0: split_weights})

        @block.tensor
        def _(pe):
            mm = nc.tensor.matmul
            tr = nc.tensor.transpose
            pe.wait_ge(c_done, 1)
            pe.wait_ge(ident_ready, 1)
            tr(ps_o[:, 0, 0:B], c_silu[:, :], ident[0:B, 0:B]).then_inc(cT_ready, 1)
            pe.wait_ge(cT_copied, 1)
            pe.wait_ge(wmod_loaded, 16)
            for n, j in enumerate((1, 0, 4, 3)):
                ins = mm(ps_o[:, 1, B * n:B * n + B], wmod_sb[:, D * j:D * j + D], cT[:, :], start=True, stop=True)
            ins.then_inc(mod_ready, 1)

            def gate_products():
                for n, j in enumerate((2, 5)):
                    ins = mm(ps_o[0:B, 0, D * n:D * n + D], cT[:, :], wmod_sb[:, D * j:D * j + D],
                             start=True, stop=True)
                ins.then_inc(mod_ready, 1)
                pe.wait_ge(mod_stored, 2)
                pe.wait_ge(consts_ready, 6)

            def x1_turn(b, _):
                if before(b) is not None:
                    pe.wait_ge(q2_copied, before(b).after(2, 2))
                pe.wait_ge(xn1_ready, b.after(NT, NT))
                for t in range(NT):
                    ins = tr(ps_f[:, t * P:t * P + P], xn1[:, t, :], ident[:, :])
                ins.then_inc(xT1_ready, 1)

            def qkv(b, t):
                if t == 0:
                    pe.wait_ge(h1_copied, b.after(1, 1))
                    if isinstance(b.i, int) and b.index == 0:
                        pe.wait_ge(weights_loaded, 16 * 4)
                else:
                    pe.wait_ge(qk_read, b.after(3 * NT, 3 * t))
                    pe.wait_ge(v_copied, b.after(2 * NT, 2 * t))
                mm(ps_f[:, 0:3 * D], h1T[:, t * P:t * P + P], wqkv_sb[:, :], start=True, stop=True
                   ).then_inc(qkv_ready, 1)

            def transpose_stack(block):
                for n in range(2):
                    for t in range(NT):
                        at = n * S + t * P
                        ins = tr(ps_f[:, at:at + P],
                                 stack[:, t, (block + n) * P:(block + n + 1) * P].bitcast(F32), ident[:, :])
                return ins

            def stack_turn(b, f):
                if f == 0:
                    pe.wait_ge(lo_done, b.after(2, 2))
                    pe.wait_ge(hi_again, b.after(2, 2))
                    pe.wait_ge(v_copied, b.after(2 * NT, 2 * NT))
                else:
                    pe.wait_ge(st_copied, b.after(4, f))
                transpose_stack((NA, NA + 2, 0, 2)[f]).then_inc(st_ready, 1)

            def shift(b, f):
                if f == 0:
                    pe.wait_ge(max_lo, b.after(1, 1))
                else:
                    pe.wait_ge(q2_copied, b.after(2, 1))
                transpose_stack(2 * f).then_inc(q2_ready, 1)

            def max_round(b, r):
                g, blocks = score_round(r)
                n, w = score_shape(r)
                if r >= 2:
                    pe.wait_ge(max_taken, b.after(NR, r - 1))
                elif before(b) is not None:
                    pe.wait_ge(exp_done, b.after(NR, r - 1))
                if r == 0:
                    pe.wait_ge(st_copied, b.after(4, 4))
                if r == 8:
                    pe.wait_ge(k_parted, b.after(NG, NG))
                view = ps_score[r % 2][:, :].rearrange("p (a q) -> p a q", a=n)
                mm(view[:, :, w - P:w], ident_b[:, :], mask_q[:, 0:n * P].rearrange("p (a q) -> p a q", a=n),
                   start=True, stop=False, skip_group_check=True)
                if g is None:
                    a = blocks[0]
                    ins = mm(view[:, :, :], qT[b.p][:, a, 0:P], k_apart[:, a, :, :], start=False, stop=True,
                             skip_group_check=True)
                else:
                    rows = slice(W * g, W * g + KS)
                    for m, a in enumerate(blocks):
                        ins = mm(view[:, m, :], qT[b.p][rows, a, P:2 * P], kT[b.p][rows, a, :],
                                 start=False, stop=m == n - 1, skip_group_check=True)
                ins.then_inc(max_scores, 1)

            def exp_round(b, r):
                g, blocks = score_round(r)
                n, w = score_shape(r)
                if r == 0:
                    pe.wait_ge(q2_copied, b.after(2, 2))
                if r == 8:
                    pe.wait_ge(q_parted, b.after(NG, NG))
                if r >= 2:
                    pe.wait_ge(exp_done, b.after(NR, r - 1))
                else:
                    pe.wait_ge(max_taken, b.after(NR, NR - 1 + r))
                if g is None:
                    a = blocks[0]
                    ins = mm(ps_score[r % 2][:, :], kT[b.p][:, a, P:2 * P],
                             q_apart[:, a, :, :].rearrange("p g q -> p (g q)"), start=True, stop=True)
                else:
                    rows = slice(W * g, W * g + KM)
                    for m, a in enumerate(blocks):
                        ins = mm(ps_score[r % 2][:, m * w:m * w + w], kT[b.p][rows, a, 0:P],
                                 qT[b.p][rows, a, :], start=m == 0, stop=m == n - 1, skip_group_check=True)
                ins.then_inc(exp_scores, 1)

            def values(b, n):
                pe.wait_ge(exp_masked, b.after(NR, rounds_of(n)[-1] + 1))
                if n == 0 and before(b) is not None:
                    pe.wait_ge(o_copied, before(b).after(1, 1))
                for r in rounds_of(n):
                    g, blocks = score_round(r)
                    w = score_shape(r)[1]
                    for m, a in enumerate(blocks):
                        if g is None:
                            m, t, row = n - 4, 1, n - 4
                        else:
                            t, row = 0, g
                        ins = mm(ps_o[W * a:W * a + W, row // 2, S - w:S], v_ones[b.p][:, t, 4 * a + row, :],
                                 probs[r % NP][:, m * w:m * w + w], start=n == 0, stop=n == NV - 1,
                                 skip_group_check=True)
                ins.then_inc(pv_done, 1)

            def o_turn(b, _):
                pe.wait_ge(o_copied, b.after(1, 1))
                if before(b) is not None:
                    pe.wait_ge(comb_steps, before(b).after(7, 4))
                for t in range(NT):
                    for j in range(2):
                        at = (2 * t + j) * P
                        ins = tr(ps_t[:, at:at + P], oT[:, j, t * P:t * P + P], ident[:, :])
                ins.then_inc(o_turned, 1)

            def on_turn(b, _):
                pe.wait_ge(on_ready, b.after(1, 1))
                for t in range(NT):
                    ins = tr(ps_t[:, t * P:t * P + P],
                             on[:, t * H:t * H + H, :].rearrange("p c d -> p (c d)"), ident[:, :])
                ins.then_inc(on_turned, 1)

            def project(b, _):
                pe.wait_ge(on_copied, b.after(1, 1))
                for t in range(NT):
                    ins = mm(ps_t[:, t * P:t * P + P], onT[:, t * P:t * P + P], wo_sb[:, :],
                             start=True, stop=True)
                ins.then_inc(wo_ready, 1)

            def x2_turn(b, _):
                pe.wait_ge(xn2_ready, b.after(NT, NT))
                for t in range(NT):
                    ins = tr(ps_t[:, t * P:t * P + P], xn2[:, t, :], ident[:, :])
                ins.then_inc(xT2_ready, 1)

            def logits(b, _):
                pe.wait_ge(h2_copied, b.after(1, 1))
                for t in range(NT):
                    ins = mm(ps_t[:, t * E:t * E + E], h2T[:, t * P:t * P + P], gw_sb[:, :],
                             start=True, stop=True)
                ins.then_inc(logits_ready, 1)

            def counts(b, _):
                pe.wait_ge(sel_ready, b.after(1, 1))
                if before(b) is not None:
                    pe.wait_ge(comb_steps, before(b).after(7, 7))
                at = ps_t[:, :]
                mm(at[:, 0:E], before_b[:, :], sel_b[:, 0, :], start=True, stop=False)
                mm(at[:, 0:E], ones_b[:, :], sel_past[:, :], start=False, stop=True)
                mm(at[:, E:2 * E], before_b[:, :], sel_b[:, 1, :], start=True, stop=False)
                mm(at[:, E:2 * E], ones_b[:, :], sel_b[:, 0, :], start=False, stop=False)
                mm(at[:, E:2 * E], ones_b[:, :], sel_past[:, :], start=False, stop=True
                   ).then_inc(counts_ready, 1)

            def gate_up(b, k):
                if k == 0:
                    pe.wait_ge(h2_lo_done, b.after(1, 1))
                    if isinstance(b.i, int) and b.index == 0:
                        pe.wait_ge(ffn_split, 2)
                if k >= 2 or before(b) is not None:
                    pe.wait_ge(hid_ready, b.after(NX, k - 1))
                for o in range(2):
                    c0 = (2 * k + o) * I
                    at = ps_gu[k % 2][:, o, :]
                    mm(at, wgu_hi[:, c0:c0 + I], h2_hi[b.p][:, :], start=True, stop=False)
                    mm(at, wgu_hi[:, c0:c0 + I], h2_lo[b.p][:, :], start=False, stop=False)
                    ins = mm(at, wgu_lo[:, c0:c0 + I], h2_hi[b.p][:, :], start=False, stop=True)
                ins.then_inc(gu_ready, 1)

            def down(b, k):
                if k < NSH:
                    pe.wait_ge(hid_ready, b.after(NX, k + 1))
                else:
                    pe.wait_ge(hid_weighed, b.after(E, k - NSH + 1))
                if k == 0 and before(b) is not None:
                    pe.wait_ge(gacc_ready, before(b).after(1, 1))
                for t in range(NT):
                    ins = mm(ps_y[:, 0, t * D:t * D + D], hid[hid_of(b, k)][:, t * P:t * P + P],
                             wd_sb[:, k * D:k * D + D], start=k == 0 and t == 0, stop=k == NX - 1,
                             skip_group_check=True)
                ins.then_inc(down_done, 1)

            run_steps(pe, "pe", {
                ("front", "x1_turn"): x1_turn, ("front", "qkv"): qkv, ("front", "stack"): stack_turn,
                ("mid", "max"): max_round, ("mid", "shift"): shift, ("mid", "exp"): exp_round,
                ("mid", "values"): values, ("tail", "o_turn"): o_turn, ("tail", "on_turn"): on_turn,
                ("tail", "wo"): project, ("tail", "x2_turn"): x2_turn, ("tail", "logits"): logits,
                ("tail", "counts"): counts, ("ffn", "gate_up"): gate_up, ("ffn", "down"): down},
                {-1: gate_products})


def kernel(L0_attn_x, L0_attn_Wq, L0_attn_Wk, L0_attn_Wv, L0_attn_Wo, L0_ffn_gate_w, L0_ffn_we_gate,
           L0_ffn_we_up, L0_ffn_we_down, L0_ffn_ws_gate, L0_ffn_ws_up, L0_ffn_ws_down, L0_c, L0_wmod):
    import concourse.bacc as bacc
    from concourse.bass_utils import run_bass_kernel_spmd

    arr = lambda a: np.asarray(a)
    inv_freq = (np.float32(1.0) / np.float32(10000.0) ** (np.arange(0, DK, 2, dtype=np.float32) / np.float32(DK)))
    theta = np.arange(S, dtype=np.float32)[:, None] * inv_freq[None, :].astype(np.float32)
    sign = np.tile(np.array([-1.0, 1.0], np.float32), DK // 2)
    rope = np.stack([np.repeat(np.cos(theta), 2, axis=-1), np.repeat(np.sin(theta), 2, axis=-1) * sign],
                    axis=1).astype(np.float32)
    wo = arr(L0_attn_Wo).reshape(NA, 2, 2, DK, D).transpose(1, 0, 2, 3, 4)
    g = np.concatenate([arr(L0_ffn_ws_gate).reshape(NSH, I, D), arr(L0_ffn_we_gate)])
    u = np.concatenate([arr(L0_ffn_ws_up).reshape(NSH, I, D), arr(L0_ffn_we_up)])
    wgu = np.stack([g, u], axis=1).transpose(3, 0, 1, 2).reshape(D, NX * 2 * I)
    d = np.concatenate([arr(L0_ffn_ws_down).reshape(D, NSH, I).transpose(1, 0, 2), arr(L0_ffn_we_down)])
    wd = d.transpose(2, 0, 1).reshape(I, NX * D)
    arrays = {
        "x": arr(L0_attn_x), "wqkv": np.concatenate([arr(L0_attn_Wq), arr(L0_attn_Wk), arr(L0_attn_Wv)], axis=1),
        "wo": wo.reshape(P, D), "gate_w": arr(L0_ffn_gate_w).T, "wgu": wgu, "wd": wd,
        "c": arr(L0_c), "wmod": arr(L0_wmod), "rope": rope,
    }
    nc = bacc.Bacc("TRN2", target_bir_lowering=False, num_devices=1)
    arrays = {f"in_{k}": np.ascontiguousarray(a) for k, a in arrays.items()}
    ins = [nc.dram_tensor(k, a.shape, F32, kind="ExternalInput").ap() for k, a in arrays.items()]
    out = nc.dram_tensor("out_0", (B, S, D), F32, kind="ExternalOutput").ap()
    block_kernel(nc, *ins, out)
    return run_bass_kernel_spmd(nc, [arrays], core_ids=[0]).results[0]["out_0"]
```
